# Optimizing a Trainium2 kernel written in Bass

```python
import numpy as np
import jax
import jax.numpy as jnp

def _softmax(x, axis=-1):
    return jax.nn.softmax(x, axis=axis)

def _gelu(x):
    return jax.nn.gelu(x, approximate=True)

def _silu(x):
    return jax.nn.silu(x)

def _sigmoid(x):
    return jax.nn.sigmoid(x)

def _layernorm(x, axis=-1, eps=1e-05):
    m = jnp.mean(x, axis=axis, keepdims=True)
    v = jnp.var(x, axis=axis, keepdims=True)
    return (x - m) / jnp.sqrt(v + eps)

def _scatter_add(tgt, idx, src, axis=0):
    return tgt.at[idx].add(src)

def _segment_sum(src, seg, n):
    return jax.ops.segment_sum(src, seg, n)
kernel_name = 'mk_gnn_preln_d2_gnn_r8_5284cc'

def setup_inputs(seed: int=0):
    np.random.seed(seed)
    _w = jnp.asarray

    def _rec_inputs():
        import jax
        import jax.numpy as jnp
        _gk = jax.random.key(seed)
        x = -0.0003713 + 1 * jax.random.normal(jax.random.fold_in(_gk, 1), (12500, 256), jnp.float32)
        src = jax.random.randint(jax.random.fold_in(_gk, 2), (200000,), 0, 12500, jnp.int32)
        dst = jnp.minimum((12500 * jax.random.uniform(jax.random.fold_in(_gk, 3), (200000,)) ** 2.0).astype(jnp.int32), 99999)
        _o = jnp.argsort(dst, stable=True)
        src = src[_o]
        dst = dst[_o]
        edge_attr_96 = -4.21973e-05 + 0.999841 * jax.random.normal(jax.random.fold_in(_gk, 12), (200000, 96), jnp.float32)
        return (x, src, dst, edge_attr_96)
    x, src, dst, edge_attr_96 = _rec_inputs()

    def _L0_gnn_setup():
        import jax, jax.numpy as jnp
        import numpy as np
        N_NODES = 6250
        N_EDGES = 100000
        EDGE_F = 96
        NODE_F = 256
        GLOB_F = 64
        HIDDEN = 1024
        N_GRAPHS = 8
        MLP_IN = NODE_F + 3 * EDGE_F + GLOB_F
        key = jax.random.key(seed)
        ks = jax.random.split(key, 9)
        x = jax.random.normal(ks[0], (N_NODES, NODE_F), dtype=jnp.float32)
        edge_attr = jax.random.normal(ks[1], (N_EDGES, EDGE_F), dtype=jnp.float32)
        u = jax.random.normal(ks[2], (N_GRAPHS, GLOB_F), dtype=jnp.float32)
        W1 = jax.random.normal(ks[3], (MLP_IN, HIDDEN), dtype=jnp.float32) * (1.0 / np.sqrt(MLP_IN))
        b1 = jax.random.normal(ks[4], (HIDDEN,), dtype=jnp.float32) * 0.01
        W2 = jax.random.normal(ks[5], (HIDDEN, NODE_F), dtype=jnp.float32) * (1.0 / np.sqrt(HIDDEN))
        b2 = jax.random.normal(ks[6], (NODE_F,), dtype=jnp.float32) * 0.01
        edge_index = jax.random.randint(ks[7], (2, N_EDGES), 0, N_NODES, dtype=jnp.int64 if jax.config.jax_enable_x64 else jnp.int32)
        batch = jnp.sort(jax.random.randint(ks[8], (N_NODES,), 0, N_GRAPHS, dtype=jnp.int32))
        return {'x': x, 'edge_attr': edge_attr, 'u': u, 'W1': W1, 'b1': b1, 'W2': W2, 'b2': b2, 'edge_index': edge_index, 'batch': batch}
    _L0_gnn_all = _L0_gnn_setup()
    _L0_gnn_in = {k: v for k, v in _L0_gnn_all.items() if k in ('u', 'W1', 'b1', 'W2', 'b2')}
    del _L0_gnn_all

    def _L1_gnn_setup():
        import jax, jax.numpy as jnp
        import numpy as np
        N = 6250
        E = 100000
        IN = 256
        HID = 64
        HEADS = 4
        OUT = 256
        NEG_SLOPE = 0.2

        def _gat_layer(x, src, dst, W, a_src, a_dst, b, heads, concat):
            n = x.shape[0]
            h = (x @ W).reshape(n, heads, -1)
            al_s = jnp.einsum('nhf,hf->nh', h, a_src)
            al_d = jnp.einsum('nhf,hf->nh', h, a_dst)
            e = jax.nn.leaky_relu(al_s[src] + al_d[dst], NEG_SLOPE)
            m = jax.lax.stop_gradient(jax.ops.segment_max(e, dst, num_segments=n))
            ex = jnp.exp(e - m[dst])
            denom = jax.ops.segment_sum(ex, dst, num_segments=n)
            alpha = ex / (denom[dst] + 1e-16)
            out = jax.ops.segment_sum(h[src] * alpha[:, :, None], dst, num_segments=n)
            out = out.reshape(n, -1) if concat else out.mean(axis=1)
            return out + b
        key = jax.random.key(seed)
        ks = jax.random.split(key, 12)
        s = 0.1
        return {'x': jax.random.normal(ks[0], (N, IN), jnp.float32), 'edge_index': jax.random.randint(ks[1], (2, E), 0, N, dtype=jnp.int32), 'W1': jax.random.normal(ks[2], (IN, HEADS * HID), jnp.float32) * s, 'att_src1': jax.random.normal(ks[3], (HEADS, HID), jnp.float32) * s, 'att_dst1': jax.random.normal(ks[4], (HEADS, HID), jnp.float32) * s, 'b1': jnp.zeros((HEADS * HID,), jnp.float32), 'W2': jax.random.normal(ks[5], (HEADS * HID, OUT), jnp.float32) * s, 'att_src2': jax.random.normal(ks[6], (1, OUT), jnp.float32) * s, 'att_dst2': jax.random.normal(ks[7], (1, OUT), jnp.float32) * s, 'b2': jnp.zeros((OUT,), jnp.float32)}
    _L1_gnn_all = _L1_gnn_setup()
    _L1_gnn_in = {k: v for k, v in _L1_gnn_all.items() if k in ('W1', 'att_src1', 'att_dst1', 'b1', 'W2', 'att_src2', 'att_dst2', 'b2')}
    del _L1_gnn_all
    return {'x': x, 'src': src, 'dst': dst, 'edge_attr_96': edge_attr_96, 'L0_gnn_u': _L0_gnn_in['u'], 'L0_gnn_W1': _L0_gnn_in['W1'], 'L0_gnn_b1': _L0_gnn_in['b1'], 'L0_gnn_W2': _L0_gnn_in['W2'], 'L0_gnn_b2': _L0_gnn_in['b2'], 'L1_gnn_W1': _L1_gnn_in['W1'], 'L1_gnn_att_src1': _L1_gnn_in['att_src1'], 'L1_gnn_att_dst1': _L1_gnn_in['att_dst1'], 'L1_gnn_b1': _L1_gnn_in['b1'], 'L1_gnn_W2': _L1_gnn_in['W2'], 'L1_gnn_att_src2': _L1_gnn_in['att_src2'], 'L1_gnn_att_dst2': _L1_gnn_in['att_dst2'], 'L1_gnn_b2': _L1_gnn_in['b2']}

def reference(x, src, dst, edge_attr_96, L0_gnn_u, L0_gnn_W1, L0_gnn_b1, L0_gnn_W2, L0_gnn_b2, L1_gnn_W1, L1_gnn_att_src1, L1_gnn_att_dst1, L1_gnn_b1, L1_gnn_W2, L1_gnn_att_src2, L1_gnn_att_dst2, L1_gnn_b2):
    import jax
    import jax.numpy as jnp

    def _L0_gnn_ref(x, edge_attr, u, W1, b1, W2, b2, edge_index, batch):
        import jax, jax.numpy as jnp
        import numpy as np
        N_NODES = 6250
        N_EDGES = 100000
        EDGE_F = 96
        NODE_F = 256
        GLOB_F = 64
        HIDDEN = 1024
        N_GRAPHS = 8
        MLP_IN = NODE_F + 3 * EDGE_F + GLOB_F
        col = edge_index[1]
        n = x.shape[0]
        out1 = jax.ops.segment_sum(edge_attr, col, num_segments=n)
        cnt = jax.ops.segment_sum(jnp.ones((edge_attr.shape[0], 1), edge_attr.dtype), col, num_segments=n)
        out2 = jax.ops.segment_max(edge_attr, col, num_segments=n)
        out2 = jnp.where(cnt > 0, out2, jnp.zeros_like(out2))
        out3 = out1 / jnp.maximum(cnt, 1.0)
        h = jnp.concatenate([x, out1, out2, out3, u[batch]], axis=1)
        h = jax.nn.relu(h @ W1 + b1) @ W2 + b2
        return h + x

    def _L1_gnn_ref(x, edge_index, W1, att_src1, att_dst1, b1, W2, att_src2, att_dst2, b2):
        import jax, jax.numpy as jnp
        import numpy as np
        N = 6250
        E = 100000
        IN = 256
        HID = 64
        HEADS = 4
        OUT = 256
        NEG_SLOPE = 0.2

        def _gat_layer(x, src, dst, W, a_src, a_dst, b, heads, concat):
            n = x.shape[0]
            h = (x @ W).reshape(n, heads, -1)
            al_s = jnp.einsum('nhf,hf->nh', h, a_src)
            al_d = jnp.einsum('nhf,hf->nh', h, a_dst)
            e = jax.nn.leaky_relu(al_s[src] + al_d[dst], NEG_SLOPE)
            m = jax.lax.stop_gradient(jax.ops.segment_max(e, dst, num_segments=n))
            ex = jnp.exp(e - m[dst])
            denom = jax.ops.segment_sum(ex, dst, num_segments=n)
            alpha = ex / (denom[dst] + 1e-16)
            out = jax.ops.segment_sum(h[src] * alpha[:, :, None], dst, num_segments=n)
            out = out.reshape(n, -1) if concat else out.mean(axis=1)
            return out + b
        n = x.shape[0]
        loop = jnp.arange(n, dtype=edge_index.dtype)
        ei = jnp.concatenate([edge_index, jnp.stack([loop, loop])], axis=1)
        src, dst = (ei[0], ei[1])
        h = _gat_layer(x, src, dst, W1, att_src1, att_dst1, b1, HEADS, True)
        h = jax.nn.elu(h)
        out = _gat_layer(h, src, dst, W2, att_src2, att_dst2, b2, 1, False)
        return out
    edge_index = jnp.stack([src, dst])
    batch0 = jnp.zeros((12500,), jnp.int32)
    h = jnp.maximum(_layernorm(x, axis=-1), 0.0)
    x = x + _L0_gnn_ref(h, edge_attr_96, L0_gnn_u, L0_gnn_W1, L0_gnn_b1, L0_gnn_W2, L0_gnn_b2, edge_index, batch0)
    h = jnp.maximum(_layernorm(x, axis=-1), 0.0)
    x = x + _L1_gnn_ref(h, edge_index, L1_gnn_W1, L1_gnn_att_src1, L1_gnn_att_dst1, L1_gnn_b1, L1_gnn_W2, L1_gnn_att_src2, L1_gnn_att_dst2, L1_gnn_b2)
    return x

_drawn_inputs = setup_inputs


def setup_inputs(seed=0):
    import zlib

    import numpy as np

    out = dict(_drawn_inputs(seed))
    spreads = {'L1_gnn_b1': (0.0, 0.1), 'L1_gnn_b2': (0.0, 0.1)}
    factors = {'L0_gnn_b1': 8.0, 'L0_gnn_b2': 8.0, 'L1_gnn_att_dst1': 3.874, 'L1_gnn_att_dst2': 5.247}
    for name, (base, spread) in spreads.items():
        noise = np.random.default_rng([zlib.crc32(name.encode()), seed]).standard_normal(out[name].shape)
        drawn = base * np.exp(spread * noise) if base else spread * noise
        out[name] = jnp.asarray(drawn.astype(out[name].dtype))
    for name, factor in factors.items():
        out[name] = (out[name] * factor).astype(out[name].dtype)
    return out
```

```python
import numpy as np
from contextlib import ExitStack, contextmanager

import concourse.bass as bass
from concourse import mybir

F32 = mybir.dt.float32
BF16 = mybir.dt.bfloat16
I32 = mybir.dt.int32
ALU = mybir.AluOpType
ACT = mybir.ActivationFunctionType
AX = mybir.AxisListType

P = 128
XF = 256
EF = 96
BIG = 1e30
PAD_NODE = 1 << 20
TB = 16
SLOTS = TB + 1
REC = 3 * SLOTS + 1


class Shapes:

    def __init__(self, nodes, edges):
        self.N, self.E = nodes, edges
        self.NT = -(-nodes // (14 * P)) * 14
        self.NP = self.NT * P
        self.NI = -(-(edges // P + self.NT) // P) * P
        self.KT = self.NI // P
        self.NB = self.NI // TB
        self.ET = -(-(self.NI - self.NT + 1) // 32) * 32
        self.EP = self.ET * P


@contextmanager
def stage(nc, tag):
    used = []

    def sem(name):
        used.append(nc.alloc_semaphore(f"{tag}_{name}"))
        return used[-1]

    with ExitStack() as c:
        yield c, sem
    nc.clear_and_free_semaphores(used)
    nc.all_engine_barrier()


class Chain:

    def __init__(self, eng, sem):
        self.eng, self.sem, self.n = eng, sem, 0

    def __call__(self, ins):
        ins.then_inc(self.sem, 1)
        self.n += 1
        self.eng.wait_ge(self.sem, self.n)


def structure(nc, s, io, dr, keep):
    NT, NP, NI, KT, NB, ET, EP = s.NT, s.NP, s.NI, s.KT, s.NB, s.ET, s.EP
    EW = EP // P
    JB = 14
    with stage(nc, "structure") as (c, sem):
        sb = lambda n, sh, dt=F32: c.enter_context(nc.sbuf_tensor(n, sh, dt))
        nat = sb("nat", [P, EW], I32)
        nat_prev = sb("nat_prev", [P, EW], I32)
        keep_sum = sb("keep_sum", [P, EW], BF16)
        keep_max = sb("keep_max", [P, EW], BF16)
        last_i = sb("last_i", [1, ET], I32)
        last_f = sb("last_f", [1, ET])
        last_all = sb("last_all", [P, ET])
        ones = sb("ones_row", [P, P])
        junk = sb("junk", [P, JB // 2, ET], BF16)
        node = sb("node", [P, NT])
        node_i = sb("node_i", [P, NT], I32)
        node_above = sb("node_above", [P, NT])
        junk_act = sb("junk_act", [P, ET], BF16)
        full = sb("full", [P, NT])
        full_i = sb("full_i", [P, NT], I32)
        rows = sb("rows", [P, 2, JB, P], I32)
        le = sb("le", [P, JB, P])
        part = sb("part", [P, NT])
        end = sb("end", [P, NT])
        endT = sb("endT", [NT, P])
        prevT = sb("prevT", [NT, P])
        cntT = sb("cntT", [NT, P])
        endm = sb("endm", [P, NT])
        shift = sb("shift", [P, P])
        shift_i = sb("shift_i", [P, P], I32)
        bi = sb("bi", [NT, 1], I32)
        lo = sb("lo", [NT, 1], I32)
        lof = sb("lof", [NT, 1])
        pidx_i = sb("pidx_i", [P, 1], I32)
        pidx = sb("pidx", [P, 1])
        tj = sb("tj", [NT, 1])
        titem = sb("titem", [P, NI], I32)
        started = sb("started", [NT, NI], BF16)
        ones_b = sb("ones_b", [P, 1], BF16)
        jrow = sb("jrow", [1, NI])
        jcol = sb("jcol", [P, KT])
        tcol = sb("tcol", [P, KT], I32)
        icol = sb("icol", [P, KT])
        icol_i = sb("icol_i", [P, KT], I32)
        base = sb("base", [P, KT])
        pp = [c.enter_context(nc.psum_tensor(f"pa{i}", [P, 512], F32)) for i in range(2)]
        loaded, masks, lasts, iotas = sem("loaded"), sem("masks"), sem("lasts"), sem("iotas")
        vec, pool_, bc, bc_used = sem("vec"), sem("pool_"), sem("bc"), sem("bc_used")
        full_ready, rows_used = sem("full_ready"), sem("rows_used")
        rows_in = [sem("rows_in0"), sem("rows_in1")]
        last_ready, counted_dve, counted_act = sem("last_ready"), sem("counted_dve"), sem("counted_act")
        t_in, t_out, stored = sem("t_in"), sem("t_out"), sem("stored")
        block = c.enter_context(nc.Block())

        @block.sync
        def _(sp):
            sp.dma_start(last_i[:, :], io["dst"].rearrange("(t e) -> t e", e=P)[:, P - 1:P]
                         .rearrange("t e -> e t"), allow_slow_non_contiguous=True).then_inc(lasts, 16)
            sp.dma_start(nat[:, :], io["dst"].rearrange("(p e) -> p e", p=P)).then_inc(loaded, 16)
            sp.dma_start(nat_prev[:, :], io["dst_prev"].rearrange("(p e) -> p e", p=P)).then_inc(loaded, 16)
            sp.wait_ge(masks, 2)
            sp.dma_start(dr["keep_sum"].rearrange("(p e) -> p e", p=P), keep_sum[:, :]).then_inc(stored, 16)
            sp.dma_start(dr["keep_max"].rearrange("(p e) -> p e", p=P), keep_max[:, :]).then_inc(stored, 16)
            sp.wait_ge(stored, 32)

        @block.gpsimd
        def _(g):
            ch = Chain(g, pool_)
            ch(g.iota(node_i[:, :], pattern=[[P, NT]], base=0, channel_multiplier=1))
            ch(g.iota(shift_i[:, :], pattern=[[1, P]], base=0, channel_multiplier=-1))
            ch(g.iota(pidx_i[:, :], pattern=[[0, 1]], base=0, channel_multiplier=1))
            ch(g.iota(titem[:, :], pattern=[[1, NI]], base=0, channel_multiplier=0))
            ch(g.iota(tcol[:, :], pattern=[[P, KT]], base=0, channel_multiplier=1))
            ch(g.memset(ones[:, :], 1.0))
            ch(g.memset(ones_b[:, :], 1.0))
            g.sem_inc(iotas, 1)
            for b in range(NT // JB):
                g.wait_ge(full_ready, b + 1)
                if b >= 2:
                    g.wait_ge(rows_used, b - 1)
                for q in range(JB):
                    g.indirect_dma_start(
                        out=rows[:, b % 2, q, :], out_offset=None, in_=io["dst"].rearrange("(t e) -> t e", e=P),
                        in_offset=bass.IndirectOffsetOnAxis(ap=full_i[:, b * JB + q:b * JB + q + 1], axis=0),
                    ).then_inc(rows_in[b % 2], 16)
            g.wait_ge(t_out, 3)
            for name, src in (("D", "dst"), ("Nx", "dst_next"), ("S", "src")):
                for k in range(KT):
                    g.indirect_dma_start(
                        out=keep[name][:, k, :], out_offset=None,
                        in_=io[src].rearrange("(t e) -> t e", e=P),
                        in_offset=bass.IndirectOffsetOnAxis(ap=icol_i[:, k:k + 1], axis=0),
                    ).then_inc(keep["items_in"], 16)
            g.wait_ge(keep["items_in"], 16 * 3 * KT)

        @block.tensor
        def _(pe):
            pe.wait_ge(iotas, 1)
            pe.wait_ge(lasts, 17)
            for i, c0 in enumerate(range(0, ET, 512)):
                w = min(512, ET - c0)
                if i >= 2:
                    pe.wait_ge(bc_used, i - 1)
                pe.matmul(pp[i % 2][:, 0:w], ones[0:1, :], last_f[0:1, c0:c0 + w], start=True, stop=True).then_inc(bc, 1)
            pe.wait_ge(t_in, 1)
            pe.transpose(pp[0][0:NT, 0:P], end[:, :], keep["ident"][:, :]).then_inc(t_out, 1)
            pe.wait_ge(t_in, 2)
            pe.matmul(pp[1][0:NT, 0:1], shift[0:NT, 0:NT], endT[:, P - 1:P], start=True, stop=True).then_inc(t_out, 1)
            pe.wait_ge(t_in, 3)
            pe.transpose(pp[0][:, 0:NT], cntT[:, :], keep["ident"][0:NT, 0:NT])
            for k in range(KT):
                pe.matmul(pp[0][:, 256 + k:257 + k], started[:, k * P:(k + 1) * P], ones_b[0:NT, :],
                          start=True, stop=True, skip_group_check=True)
            for i, c0 in enumerate(range(0, NI, 512)):
                w = min(512, NI - c0)
                pe.wait_ge(t_in, 3 + i)
                pe.matmul(pp[1][0:1, 0:w], ones_b[0:NT, :], started[:, c0:c0 + w],
                          start=True, stop=True).then_inc(bc, 1)

        @block.scalar
        def _(a):
            a.wait_ge(last_ready, 1)
            for j in range(1, NT, 2):
                if j > 1:
                    a.wait_ge(counted_act, j // 2)
                a.activation(junk_act[:, :], last_all[:, :], ACT.Sign, bias=node_above[:, j:j + 1], scale=-1.0,
                             accum_out=full[:, j:j + 1]).then_inc(counted_act, 1)

        @block.vector
        def _(v):
            ch = Chain(v, vec)
            v.wait_ge(lasts, 16)
            ch(v.tensor_copy(last_f[:, :], last_i[:, :]))
            v.sem_inc(lasts, 1)
            v.wait_ge(loaded, 32)
            v.wait_ge(iotas, 1)
            v.tensor_tensor(keep_sum[:, :], nat[:, :], nat_prev[:, :], ALU.is_equal).then_inc(masks, 1)
            v.wait_ge(masks, 1)
            v.tensor_scalar(keep_max[:, :], keep_sum[:, :], -1.0, BIG, ALU.add, ALU.mult).then_inc(masks, 1)
            ch(v.tensor_copy(node[:, :], node_i[:, :]))
            ch(v.tensor_scalar(node_above[:, :], node_i[:, :], 0.5, None, ALU.add))
            ch(v.tensor_copy(pidx[:, :], pidx_i[:, :]))
            ch(v.tensor_scalar(shift[:, :], shift_i[:, :], 1.0, None, ALU.is_equal))
            nbc = 0
            for i, c0 in enumerate(range(0, ET, 512)):
                w = min(512, ET - c0)
                v.wait_ge(bc, i + 1)
                v.tensor_copy(last_all[:, c0:c0 + w], pp[i % 2][:, 0:w]).then_inc(bc_used, 1)
                nbc += 1
            v.wait_ge(bc_used, nbc)
            v.sem_inc(last_ready, 1)

            def count_tiles(b):
                js = slice(b * JB, (b + 1) * JB)
                for q in range(0, JB, 2):
                    j = b * JB + q
                    v.tensor_scalar(junk[:, q // 2, :], last_all[:, :], node[:, j:j + 1], 0.0, ALU.is_le, ALU.add,
                                    accum_out=full[:, j:j + 1]).then_inc(counted_dve, 1)
                v.wait_ge(counted_act, (b + 1) * (JB // 2))
                signs = full[:, b * JB + 1:(b + 1) * JB:2]
                v.tensor_scalar(signs, signs, 0.5, ET / 2, ALU.mult, ALU.add).then_inc(counted_dve, 1)
                v.wait_ge(counted_dve, (b + 1) * (JB // 2 + 1))
                v.tensor_copy(full_i[:, js], full[:, js]).then_inc(full_ready, 1)

            def count_edges(b):
                js = slice(b * JB, (b + 1) * JB)
                v.wait_ge(rows_in[b % 2], 16 * JB * (b // 2 + 1))
                v.tensor_tensor(le[:, :, :], rows[:, b % 2, :, :], node[:, js].unsqueeze(2).to_broadcast([P, JB, P]),
                                ALU.is_le).then_inc(rows_used, 1)
                v.wait_ge(rows_used, b + 1)
                ch(v.tensor_reduce(part[:, js], le[:, :, :], AX.X, ALU.add))

            for b in range(NT // JB):
                count_tiles(b)
                if b:
                    count_edges(b - 1)
            count_edges(NT // JB - 1)
            ch(v.scalar_tensor_tensor(out=end[:, :], in0=full[:, :], scalar=float(P), in1=part[:, :],
                                      op0=ALU.mult, op1=ALU.add))
            v.sem_inc(t_in, 1)
            v.wait_ge(t_out, 1)
            ch(v.tensor_copy(endT[:, :], pp[0][0:NT, 0:P]))
            v.sem_inc(t_in, 1)
            ch(v.tensor_copy(prevT[:, 1:P], endT[:, 0:P - 1]))
            v.wait_ge(t_out, 2)
            ch(v.tensor_copy(prevT[:, 0:1], pp[1][0:NT, 0:1]))
            ch(v.tensor_tensor(cntT[:, :], endT[:, :], prevT[:, :], ALU.subtract))
            ch(v.tensor_copy(bi[:, :], prevT[:, 0:1]))
            ch(v.tensor_scalar(lo[:, :], bi[:, :], 7, None, ALU.arith_shift_right))
            ch(v.tensor_copy(lof[:, :], lo[:, :]))
            ch(v.tensor_tensor(tj[:, :], lof[:, :], pidx[0:NT, :], ALU.add))
            ch(v.tensor_scalar(started[:, :], titem[0:NT, :], tj[:, :], None, ALU.is_ge))
            v.sem_inc(t_in, 1)
            for i, c0 in enumerate(range(0, NI, 512)):
                w = min(512, NI - c0)
                v.wait_ge(bc, nbc + i + 1)
                ch(v.tensor_scalar(jrow[:, c0:c0 + w], pp[1][0:1, 0:w], -1.0, None, ALU.add))
                v.sem_inc(t_in, 1)
            ch(v.tensor_copy(keep["jrow"][:, :], jrow[:, :]))
            ch(v.tensor_copy(keep["cnt"][:, :], pp[0][:, 0:NT]))
            ch(v.tensor_scalar(jcol[:, :], pp[0][:, 256:256 + KT], -1.0, None, ALU.add))
            ch(v.tensor_tensor(icol[:, :], tcol[:, :], jcol[:, :], ALU.subtract))
            ch(v.tensor_copy(icol_i[:, :], icol[:, :]))
            ch(v.tensor_scalar(keep["base"][:, :], jcol[:, :], float(P), None, ALU.mult))
            ch(v.tensor_scalar(endm[:, :], end[:, :], -1.0, 0.0, ALU.add, ALU.max))
            ch(v.tensor_copy(keep["end_i"][:, :], endm[:, :]))
            v.sem_inc(t_out, 1)


def masks(nc, s, dr, keep):
    NI, KT, NB = s.NI, s.KT, s.NB
    with stage(nc, "masks") as (c, sem):
        sb = lambda n, sh, dt=F32: c.enter_context(nc.sbuf_tensor(n, sh, dt))
        D, Nx, S = keep["D"], keep["Nx"], keep["S"]
        d = sb("d", [P, KT, P])
        rel = sb("rel", [P, KT, P])
        clip = sb("clip", [P, KT, P])
        isl = sb("isl", [P, KT, P])
        srcf = sb("srcf", [P, KT, P])
        tab = sb("tab", [P, KT, 5, P])
        ends = sb("ends", [P, 3, KT])
        endsT = sb("endsT", [KT, 3, P])
        rowt = sb("rowt", [1, 3, NI])
        same = sb("same", [1, NI])
        cont = sb("cont", [1, NI])
        both = sb("both", [1, NI])
        rec = sb("rec", [1, NB, REC])
        pt = [c.enter_context(nc.psum_tensor(f"pt{i}", [P, 4, P], F32)) for i in range(4)]
        vec, tr, evac, stored, ready, seg = sem("vec2"), sem("tr"), sem("evac"), sem("stored2"), sem("ready"), sem("seg")
        block = c.enter_context(nc.Block())
        groups = [(q, k0, min(4, KT - k0)) for q in range(3) for k0 in range(0, KT, 4)]

        @block.vector
        def _(v):
            ch = Chain(v, vec)
            ch(v.tensor_copy(d[:, :, :], D[:, :, :]))
            ch(v.tensor_tensor(rel[:, :, :], d[:, :, :], keep["base"][:, :].unsqueeze(2).to_broadcast([P, KT, P]),
                               ALU.subtract))
            ch(v.tensor_tensor(isl[:, :, :], D[:, :, :], Nx[:, :, :], ALU.not_equal))
            ch(v.tensor_copy(srcf[:, :, :], S[:, :, :]))
            v.sem_inc(ready, 1)
            ch(v.tensor_scalar(clip[:, :, :], rel[:, :, :], 0.0, float(P - 1), ALU.max, ALU.min))
            for m, a, b, lo_, hi in ((0, d[:, :, 1:P], d[:, :, 0:P - 1], 1, P),
                                     (1, d[:, :, 0:P - 1], d[:, :, 1:P], 0, P - 1),
                                     (2, d[:, :, :], d[:, :, 0:1].to_broadcast([P, KT, P]), 0, P),
                                     (3, d[:, :, :], d[:, :, P - 1:P].to_broadcast([P, KT, P]), 0, P),
                                     (4, clip[:, :, :], rel[:, :, :], 0, P)):
                ch(v.tensor_tensor(tab[:, :, m, lo_:hi], a, b, ALU.not_equal))
            ch(v.memset(tab[:, :, 0, 0:1], 1.0))
            ch(v.memset(tab[:, :, 1, P - 1:P], 1.0))
            ch(v.tensor_scalar(tab[:, :, :, :].rearrange("p k m e -> p (k m e)"),
                               tab[:, :, :, :].rearrange("p k m e -> p (k m e)"), -BIG, None, ALU.mult))
            ch(v.tensor_copy(ends[:, 0, :], d[:, :, 0]))
            ch(v.tensor_copy(ends[:, 1, :], d[:, :, P - 1]))
            ch(v.tensor_copy(ends[:, 2, :], rel[:, :, 0]))
            v.sem_inc(ready, 1)
            for n, (q, k0, w) in enumerate(groups):
                v.wait_ge(tr, n + 1)
                out = (keep["rel"], keep["last"], keep["src"])[q]
                v.tensor_copy(out[:, k0 * P:(k0 + w) * P],
                              pt[n % 3][:, 0:w, :].rearrange("p k e -> p (k e)")).then_inc(evac, 1)
            v.wait_ge(tr, len(groups) + 1)
            ch(v.tensor_copy(endsT[:, :, :], pt[3][0:KT, 0:3, :]))
            v.sem_inc(ready, 1)
            v.wait_ge(seg, 16)
            df, dl, r0 = rowt[:, 0, :], rowt[:, 1, :], rowt[:, 2, :]
            ch(v.memset(cont[:, 0:1], 0.0))
            ch(v.tensor_tensor(cont[:, 1:NI], df[:, 1:NI], dl[:, 0:NI - 1], ALU.is_equal))
            ch(v.tensor_tensor(same[:, :], df, dl, ALU.is_equal))
            ch(v.memset(rec[:, :, :], 0.0))
            c3 = cont[:, :].rearrange("o (b t) -> o b t", t=TB)
            s3 = same[:, :].rearrange("o (b t) -> o b t", t=TB)
            ch(v.tensor_tensor(rec[:, :, 1:SLOTS], c3, s3, ALU.mult))
            ch(v.tensor_tensor(rec[:, :, SLOTS:2 * SLOTS - 2], c3[:, :, 1:TB], s3[:, :, 0:TB - 1], ALU.mult))
            ch(v.tensor_copy(rec[:, :, 2 * SLOTS:3 * SLOTS - 1], c3))
            ch(v.tensor_scalar(rec[:, :, :], rec[:, :, :], -1.0, BIG, ALU.add, ALU.mult))
            r3 = r0.rearrange("o (b t) -> o b t", t=TB)[:, :, 0:1]
            ch(v.tensor_scalar(both[:, 0:NB].unsqueeze(2), r3, 1.0, None, ALU.add))
            ch(v.tensor_tensor(both[:, 0:NB].unsqueeze(2), both[:, 0:NB].unsqueeze(2), c3[:, :, 0:1], ALU.mult))
            ch(v.tensor_scalar(rec[:, :, REC - 1:REC], both[:, 0:NB].unsqueeze(2), -1.0, None, ALU.add))
            v.sem_inc(ready, 1)

        @block.tensor
        def _(pe):
            pe.wait_ge(ready, 1)
            for n, (q, k0, w) in enumerate(groups):
                if n >= 3:
                    pe.wait_ge(evac, n - 2)
                for k in range(k0, k0 + w):
                    mm = pe.transpose(pt[n % 3][:, k - k0, :], (rel, isl, srcf)[q][:, k, :], keep["ident"][:, :])
                mm.then_inc(tr, 1)
            pe.wait_ge(ready, 2)
            for m in range(3):
                mm = pe.transpose(pt[3][0:KT, m, :], ends[:, m, :], keep["ident"][:, :])
            mm.then_inc(tr, 1)

        @block.sync
        def _(sp):
            sp.wait_ge(ready, 2)
            sp.dma_start(dr["tab"].rearrange("(k p) f -> p k f", p=P),
                         tab[:, :, :, :].rearrange("p k m e -> p k (m e)")).then_inc(stored, 16)
            sp.wait_ge(ready, 3)
            sp.dma_start(dr["ends"].rearrange("m (k p) -> k m p", p=P), endsT[:, :, :]).then_inc(stored, 16)
            sp.wait_ge(stored, 32)
            sp.dma_start(rowt[:, :, :], dr["ends"].unsqueeze(0)).then_inc(seg, 16)
            sp.wait_ge(ready, 4)
            sp.dma_start(dr["rec"].unsqueeze(0), rec[:, :, :]).then_inc(stored, 16)
            sp.wait_ge(stored, 48)


def node_tiles(nc, eng, s, keep, b):
    return nc.values_load_multi_w_load_instructions(
        keep["jrow"][0:1, bass.ds(b * TB, TB)], engines=(eng.engine,), min_val=0, max_val=s.NT - 1,
        skip_runtime_bounds_check_because="an item's node tile is a count of tiles begun, NT at most")[1]


def over_batches(eng, NB, step):
    step(-1, 1, agg=False)
    with eng.Fori(0, (NB - 2) // 2) as turn:
        for par in (0, 1):
            step(turn, par)
    step((NB - 2) // 2, 0, ahead=False)
    step((NB - 2) // 2, 1, chain=False, ahead=False)


def attention(nc, s, H, keep, dr, table, acc, adt):
    NT, NI, NB = s.NT, s.NI, s.NB
    W = XF + 2 * H
    HT = H * TB
    D = XF // H
    G = 4
    DG = 3 if H > 1 else 1
    AT = (3, 6, 6, 10, 10, 13, 16, 16)
    DV = (0, 2, 3, 9, 13)
    with stage(nc, f"attention{H}") as (c, sem):
        sb = lambda n, sh, dt=F32: c.enter_context(nc.sbuf_tensor(f"{n}{H}", sh, dt))
        rows = sb("rows_", [P, 2, TB, W])
        onehot = sb("onehot_", [P, 2, TB, P])
        narrow = sb("narrow_", [P, TB, P], BF16)
        onehotT = sb("onehotT_", [P, TB, P], BF16)
        idx = sb("idx_", [P, 2, TB], I32)
        tab = sb("tab_", [HT, 2, 5, P])
        ad = sb("ad_", [P, TB, H])
        z0 = sb("z0_", [P, TB, H])
        z = sb("z_", [P, H, TB])
        zt = sb("zt_", [HT, P])
        fwd = sb("fwd_", [HT, P])
        loc = sb("loc_", [HT, P])
        m1 = sb("m1_", [HT, P])
        mx = sb("mx_", [HT, P])
        zm = sb("zm_", [HT, P])
        wt = sb("wt_", [HT, P])
        recs = sb("recs_", [1, 2, 3, H, SLOTS])
        carried = sb("carried_", [1, 2])
        lrow = sb("lrow_", [1, H, SLOTS])
        arow = sb("arow_", [1, H, SLOTS])
        R = sb("R_", [1, H, SLOTS])
        Q = sb("Q_", [1, H, SLOTS])
        cd = sb("cd_", [1, 2, H, TB])
        mf = sb("mf_", [1, H])
        fa = sb("fa_", [1, H])
        fe = sb("fe_", [1, H])
        hot = sb("hot_", [1, 2, P])
        scale = sb("scale_", [P, 2, H])
        pT = c.enter_context(nc.psum_tensor(f"pT{H}", [P, TB // 2, P], BF16))
        pD = c.enter_context(nc.psum_tensor(f"pD{H}", [P, 512], F32))
        pA = c.enter_context(nc.psum_tensor(f"pA{H}", [P, 512], F32))
        pS = c.enter_context(nc.psum_tensor(f"pS{H}", [P, 512], F32))
        pG = [c.enter_context(nc.psum_tensor(f"pG{i}{H}", [P, 512], F32)) for i in range(4)]
        pAD = pD[:, 0:3 * HT].rearrange("p (t m h) -> p t m h", m=3, h=H)
        pW = pA[:, 0:2 * HT].rearrange("p (m h t) -> p m h t", m=2, h=H)
        psF = pA[:, 400:400 + H]
        psZ, psE, psC = pS[0:HT, 0:P], pS[0:1, P:P + 2 * HT], pS[0:HT, 300:302]
        gath_in = [sem("gath_in0"), sem("gath_in1")]
        idx_in = [sem("idx_in0"), sem("idx_in1")]
        tabs_in = [sem("tabs_in0"), sem("tabs_in1")]
        tabs_used, onehot_ready, pT_ready, pT_copied = sem("tabs_used"), sem("onehot_ready"), sem("pT_ready"), sem("pT_copied")
        ad_ready, z_ready, zT_ready, loc_ready = sem("ad_ready"), sem("z_ready"), sem("zT_ready"), sem("loc_ready")
        edge_ready, cd_ready, fexp_ready, cols_ready = sem("edge_ready"), sem("cd_ready"), sem("fexp_ready"), sem("cols_ready")
        scale_ready, zm_ready, wt_ready, w_rows = sem("scale_ready"), sem("zm_ready"), sem("wt_ready"), sem("w_rows")
        w_copied, max_copied, aggregated = sem("w_copied"), sem("max_copied"), sem("aggregated")
        weighed_dve, weighed_act = sem("weighed_dve"), sem("weighed_act")
        wide_ready, ad_summed = sem("wide_ready"), sem("ad_summed")
        added, rescaled, grown, vec = sem("added"), sem("rescaled"), sem("grown"), sem("vec_")
        pool_passed, pe_passed = sem("pool_passed"), sem("pe_passed")
        TAB_DMAS = 16 * (H + 2)
        block = c.enter_context(nc.Block())

        @block.sync
        def _(sp):
            def load(b, par, turn):
                if turn is not None:
                    sp.wait_ge(gath_in[par], turn * 16 * TB + 16 * TB)
                sp.dma_start(idx[:, par, :], keep["src"][:, bass.ds(b * TB, TB)]).then_inc(idx_in[par], 16)
                if turn is not None:
                    sp.wait_ge(tabs_used, b - 1)
                for h in range(H):
                    sp.dma_start(tab[h * TB:(h + 1) * TB, par, :, :].rearrange("t m e -> t (m e)"),
                                 dr["tab"][bass.ds(b * TB, TB), :]).then_inc(tabs_in[par], 16)
                rec = dr["rec"][bass.ds(b, 1), :]
                sp.dma_start(recs[:, par, :, :, :],
                             rec[:, 0:3 * SLOTS].rearrange("o (m k) -> o m k", m=3).unsqueeze(2)
                             .to_broadcast([1, 3, H, SLOTS])).then_inc(tabs_in[par], 16)
                sp.dma_start(carried[:, par:par + 1], rec[:, REC - 1:REC]).then_inc(tabs_in[par], 16)

            load(0, 0, None)
            load(1, 1, None)
            with sp.Fori(0, (NB - 2) // 2) as turn:
                for par in (0, 1):
                    load(turn * 2 + (2 + par), par, turn)

        @block.gpsimd
        def _(g):
            def gather(par, turn):
                g.wait_ge(idx_in[par], 16 if turn is None else turn * 16 + 32)
                for k in range(TB):
                    if turn is not None:
                        g.wait_ge(aggregated, turn * 2 * TB + (par * TB + k + 1))
                        g.sem_inc(pool_passed, 1)
                    g.indirect_dma_start(
                        out=rows[:, par, k, 0:XF + H], out_offset=None, in_=table,
                        in_offset=bass.IndirectOffsetOnAxis(ap=idx[:, par, k:k + 1], axis=0),
                    ).then_inc(gath_in[par], 16)

            gather(0, None)
            gather(1, None)
            with g.Fori(0, (NB - 2) // 2) as turn:
                for par in (0, 1):
                    gather(par, turn)

        @block.tensor
        def _(pe):
            def turn_onehots(m, half):
                if half == 0:
                    pe.wait_ge(onehot_ready, m + 1)
                pe.wait_ge(pT_copied, m * 2 + (half + 1))
                for k in range(TB // 2):
                    mm = pe.transpose(pT[:, k, :], narrow[:, half * (TB // 2) + k, :], keep["ident_b"][:, :])
                mm.then_inc(pT_ready, 1)

            def destinations(m, tiles):
                pe.wait_ge(z_ready, m + 1)
                for k in range(TB):
                    if k % (TB // 2) == 0:
                        pe.wait_ge(pT_copied, m * 2 + (k // (TB // 2) + 2))
                    mm = pe.matmul(pAD[:, k, :, :].rearrange("p m h -> p (m h)"), onehotT[:, k, :],
                                   adt[:, bass.ds(tiles[k], 1), :, :].rearrange("p o m h -> p (o m h)"),
                                   start=True, stop=True, skip_group_check=True)
                mm.then_inc(ad_ready, 1)

            def aggregate(b, par, ks):
                for k in ks:
                    if k == 0:
                        pe.wait_ge(wide_ready, b + 1)
                    if k % G == 0 and k < DG * G:
                        pe.wait_ge(weighed_dve, b * DG + (k // G + 1))
                    elif k >= DG * G:
                        pe.wait_ge(weighed_act, b * (TB - DG * G) + (k - DG * G + 1))
                    pe.wait_ge(added, b * TB + (k + 1))
                    pe.matmul(pG[k % 4][:, 0:W], onehot[:, par, k, :], rows[:, par, k, :],
                              start=True, stop=True).then_inc(aggregated, 1)

            def step(turn, par, agg=True, chain=True, ahead=True):
                b, n = turn * 2 + par, turn * 2 + (par + 1)
                part = lambda i: aggregate(b, par, range(AT[i - 1] if i else 0, AT[i])) if agg else None
                if ahead:
                    tiles = node_tiles(nc, pe, s, keep, n + 1)
                part(0)
                if chain:
                    pe.wait_ge(z_ready, n + 2)
                    pe.sem_inc(pe_passed, 1)
                    pe.transpose(psZ, z[:, :, :].rearrange("p h t -> p (h t)"),
                                 keep["ident"][:, :]).then_inc(zT_ready, 1)
                part(1)
                if chain:
                    pe.wait_ge(loc_ready, n + 1)
                    pe.sem_inc(pe_passed, 1)
                    pe.transpose(psE[:, 0:HT], loc[:, 0:1], keep["ident"][0:HT, 0:HT])
                    pe.transpose(psE[:, HT:2 * HT], loc[:, P - 1:P],
                                 keep["ident"][0:HT, 0:HT]).then_inc(edge_ready, 1)
                part(2)
                if ahead:
                    turn_onehots(n + 1, 0)
                part(3)
                if chain:
                    pe.wait_ge(cd_ready, n + 1)
                    pe.sem_inc(pe_passed, 1)
                    pe.transpose(psC[:, 0:1], cd[:, 0, :, :].rearrange("o h t -> o (h t)"), keep["ident"][0:1, 0:1])
                    pe.transpose(psC[:, 1:2], cd[:, 1, :, :].rearrange("o h t -> o (h t)"),
                                 keep["ident"][0:1, 0:1]).then_inc(cols_ready, 1)
                part(4)
                if chain:
                    pe.wait_ge(fexp_ready, n + 1)
                    pe.wait_ge(max_copied, n + 1)
                    pe.sem_inc(pe_passed, 1)
                    pe.matmul(psF, hot[:, 0, :], fe[:, :], start=True, stop=False, skip_group_check=True)
                    pe.matmul(psF, hot[:, 1, :], keep["ones"][0:1, 0:H], start=False, stop=True,
                              skip_group_check=True).then_inc(cols_ready, 1)
                if ahead:
                    turn_onehots(n + 1, 1)
                part(5)
                if chain:
                    pe.wait_ge(wt_ready, n + 1)
                    pe.wait_ge(scale_ready, n + 1)
                    pe.sem_inc(pe_passed, 1)
                    pe.transpose(pW[:, 0, :, :].rearrange("p h t -> p (h t)"), wt[:, :], keep["ident"][0:HT, 0:HT])
                    pe.transpose(pW[:, 1, :, :].rearrange("p h t -> p (h t)"), mx[:, :],
                                 keep["ident"][0:HT, 0:HT]).then_inc(w_rows, 1)
                part(6)
                if ahead:
                    destinations(n + 1, tiles)
                part(7)

            pe.sem_inc(cols_ready, 1)
            pe.sem_inc(w_rows, 1)
            turn_onehots(0, 0)
            turn_onehots(0, 1)
            destinations(0, node_tiles(nc, pe, s, keep, 0))
            over_batches(pe, NB, step)

        @block.scalar
        def _(a):
            def turned(m, half, first=False):
                a.wait_ge(pT_ready, m * 2 + (half + 1))
                if half == 0 and not first:
                    a.wait_ge(ad_ready, m)
                a.activation(onehotT[:, half * (TB // 2):(half + 1) * (TB // 2), :].rearrange("p k e -> p (k e)"),
                             pT[:, :, :].rearrange("p k e -> p (k e)"), ACT.Copy).then_inc(pT_copied, 1)

            def widen(m, par, first=False):
                if not first:
                    a.wait_ge(aggregated, (m - 1) * TB)
                a.activation(onehot[:, par, :, :].rearrange("p k e -> p (k e)"),
                             narrow[:, :, :].rearrange("p k e -> p (k e)"), ACT.Copy).then_inc(wide_ready, 1)

            def step(n, par, ahead=True):
                if ahead:
                    turned(n + 1, 0)
                a.wait_ge(cd_ready, n + 1)
                a.wait_ge(cols_ready, n * 2 + 1)
                a.activation(fe[:, :], fa[:, :], ACT.Exp).then_inc(fexp_ready, 1)
                a.wait_ge(cols_ready, n * 2 + 3)
                a.activation(scale[:, par, :], psF, ACT.Copy).then_inc(scale_ready, 1)
                if ahead:
                    turned(n + 1, 1)
                a.wait_ge(zm_ready, n + 1)
                a.wait_ge(w_rows, n + 1)
                a.activation(wt[:, :], zm[:, :], ACT.Exp).then_inc(wt_ready, 1)
                a.wait_ge(w_rows, n + 2)
                a.activation(rows[:, par, :, XF:XF + H], pW[:, 0, :, :].rearrange("p h t -> p t h"),
                             ACT.Copy).then_inc(w_copied, 1)
                a.wait_ge(w_copied, n + 1)
                for k in range(DG * G, TB):
                    for h in range(H):
                        at = rows[:, par, k, h * D:(h + 1) * D]
                        ins = a.activation(at, at, ACT.Copy, scale=rows[:, par, k, XF + h:XF + h + 1])
                    ins.then_inc(weighed_act, 1)
                if ahead:
                    widen(n + 1, 1 - par)

            a.sem_inc(pT_copied, 1)
            turned(0, 0, first=True)
            turned(0, 1, first=True)
            widen(0, 0, first=True)
            step(0, 0)
            with a.Fori(0, (NB - 2) // 2) as turn:
                step(turn * 2 + 1, 1)
                step(turn * 2 + 2, 0)
            step(NB - 1, 1, ahead=False)

        @block.vector
        def _(v):
            OPS = 12

            def onehots(m, first=False):
                if not first:
                    v.wait_ge(wide_ready, m)
                v.tensor_tensor(narrow[:, :, :],
                                keep["iota"][:, :].unsqueeze(1).to_broadcast([P, TB, P]),
                                keep["rel"][:, bass.ds(m * TB, TB)].unsqueeze(2).to_broadcast([P, TB, P]),
                                ALU.is_equal).then_inc(onehot_ready, 1)

            def linked(n, between):
                def done(ins, k):
                    ins.then_inc(vec, 1)
                    between()
                    v.wait_ge(vec, n * OPS + (k + 2))
                return done

            def scores(n, par, half, between):
                done = linked(n, between)
                v.wait_ge(ad_ready, n + 1)
                v.tensor_reduce(ad[:, :, :].unsqueeze(3), pAD.rearrange("p t m h -> p t h m"),
                                AX.X, ALU.add).then_inc(ad_summed, 1)
                between()
                v.wait_ge(ad_summed, n + 1)
                v.wait_ge(gath_in[par], half * 16 * TB + 16 * TB)
                done(v.tensor_tensor(z0[:, :, :], rows[:, par, :, XF:XF + H], ad[:, :, :], ALU.add), 1)
                zv = z0[:, :, :].rearrange("p t h -> p h t")
                v.scalar_tensor_tensor(out=z[:, :, :], in0=zv, scalar=0.2, in1=zv,
                                       op0=ALU.mult, op1=ALU.max).then_inc(z_ready, 1)

            def local_maxima(n, par, half, between):
                done = linked(n, between)
                v.wait_ge(tabs_in[par], half * TAB_DMAS + TAB_DMAS)
                v.wait_ge(zT_ready, n + 1)
                done(v.tensor_tensor(zt[:, :], psZ, tab[:, par, 4, :], ALU.add), 2)
                done(v.tensor_tensor_scan(fwd[:, :], tab[:, par, 0, :], zt[:, :], -BIG, ALU.add, ALU.max), 3)
                v.tensor_tensor_scan(loc[:, ::-1], tab[:, par, 1, ::-1], fwd[:, ::-1], -BIG,
                                     ALU.add, ALU.max).then_inc(loc_ready, 1)

            def carries(n, par, between):
                done = linked(n, between)
                row = lambda x: x.rearrange("o h k -> o (h k)")
                v.wait_ge(edge_ready, n + 1)
                v.wait_ge(cols_ready, n * 2 + 1)
                v.tensor_copy(lrow[:, :, 0:1], R[:, :, TB:SLOTS]).then_inc(vec, 1)
                v.tensor_copy(arow[:, :, 0:TB], psE[:, 0:HT].rearrange("o (h t) -> o h t", h=H)).then_inc(vec, 1)
                done(v.tensor_copy(lrow[:, :, 1:SLOTS], psE[:, HT:2 * HT].rearrange("o (h t) -> o h t", h=H)), 6)
                v.tensor_tensor_scan(row(R[:, :, :]), row(recs[:, par, 0, :, :]), row(lrow[:, :, :]), -BIG,
                                     ALU.add, ALU.max).then_inc(vec, 1)
                done(v.tensor_tensor_scan(row(Q[:, :, :])[:, ::-1], row(recs[:, par, 1, :, :])[:, ::-1],
                                          row(arow[:, :, :])[:, ::-1], -BIG, ALU.add, ALU.max), 8)
                v.tensor_tensor(cd[:, 0, :, :], R[:, :, 0:TB], recs[:, par, 2, :, 0:TB], ALU.add).then_inc(vec, 1)
                v.tensor_tensor(cd[:, 1, :, :], Q[:, :, 1:SLOTS], recs[:, par, 2, :, 1:SLOTS], ALU.add).then_inc(vec, 1)
                v.tensor_scalar(hot[:, 0, :], keep["iota"][0:1, :], carried[:, par:par + 1], None, ALU.is_equal)
                v.tensor_scalar(hot[:, 1, :], keep["iota"][0:1, :], carried[:, par:par + 1], None, ALU.not_equal)
                v.wait_ge(vec, n * OPS + 12)
                done(v.tensor_tensor(mf[:, :].unsqueeze(2), Q[:, :, 0:1], cd[:, 0, :, 0:1], ALU.max), 11)
                done(v.tensor_tensor(mf[:, :].unsqueeze(2), lrow[:, :, 0:1], mf[:, :].unsqueeze(2), ALU.subtract), 12)
                v.tensor_scalar(fa[:, :], mf[:, :], 0.0, None, ALU.min).then_inc(cd_ready, 1)

            def maxima(n, par, between):
                v.wait_ge(cols_ready, n * 2 + 2)
                v.scalar_tensor_tensor(out=m1[:, :], in0=tab[:, par, 2, :], scalar=psC[:, 0:1], in1=loc[:, :],
                                       op0=ALU.add, op1=ALU.max).then_inc(grown, 1)
                between()
                v.wait_ge(grown, n * 2 + 1)
                v.scalar_tensor_tensor(out=mx[:, :], in0=tab[:, par, 3, :], scalar=psC[:, 1:2], in1=m1[:, :],
                                       op0=ALU.add, op1=ALU.max).then_inc(grown, 1)
                between()
                v.wait_ge(grown, n * 2 + 2)
                v.tensor_tensor(zm[:, :], zt[:, :], mx[:, :], ALU.subtract).then_inc(zm_ready, 1)
                between()
                v.wait_ge(zm_ready, n + 1)
                v.sem_inc(tabs_used, 1)

            def weight(n, par):
                v.wait_ge(w_copied, n + 1)
                v.tensor_tensor(rows[:, par, :, XF + H:W], pW[:, 1, :, :].rearrange("p h t -> p t h"),
                                keep["last"][:, bass.ds(n * TB, TB)].unsqueeze(2).to_broadcast([P, TB, H]),
                                ALU.mult).then_inc(max_copied, 1)

            def weigh(par, q):
                part = rows[:, par, 4 * q:4 * q + 4, 0:XF].rearrange("p k (h d) -> p k h d", h=H)
                by = rows[:, par, 4 * q:4 * q + 4, XF:XF + H].unsqueeze(3).to_broadcast([P, 4, H, D])
                v.tensor_tensor(part, part, by, ALU.mult).then_inc(weighed_dve, 1)

            def rescale(b, par, tile):
                v.wait_ge(scale_ready, b + 1)
                v.wait_ge(added, b * TB + 4)
                at = acc[:, bass.ds(tile, 1), 0:XF].rearrange("p o (h d) -> p (o h) d", h=H)
                v.tensor_tensor(at, at, scale[:, par, :].unsqueeze(2).to_broadcast([P, H, D]),
                                ALU.mult).then_inc(rescaled, 1)
                at = acc[:, bass.ds(tile, 1), XF:XF + H].rearrange("p o h -> p (o h)")
                v.tensor_tensor(at, at, scale[:, par, :], ALU.mult).then_inc(rescaled, 1)
                v.wait_ge(rescaled, b * 2 + 2)

            def add(b, par, tiles, k):
                v.wait_ge(aggregated, b * TB + (k + 1))
                if k:
                    v.wait_ge(added, b * TB + (k + 4))
                at = acc[:, bass.ds(tiles[k], 1), 0:W].rearrange("p o w -> p (o w)")
                v.tensor_tensor(at, at, pG[k % 4][:, 0:W], ALU.add).then_inc(added, 1)

            def step(turn, par, agg=True, chain=True, ahead=True):
                b, n, npar, half = turn * 2 + par, turn * 2 + (par + 1), 1 - par, turn + par
                tiles = node_tiles(nc, v, s, keep, b) if agg else None
                todo = list(range(TB)) if agg else []

                def between(upto=TB):
                    if todo and todo[0] < upto:
                        add(b, par, tiles, todo.pop(0))

                def sums(upto):
                    while todo and todo[0] < upto:
                        between()

                if agg:
                    rescale(b, par, tiles[0])
                sums(DV[0])
                if chain:
                    scores(n, npar, half, between)
                sums(DV[1])
                if ahead:
                    onehots(n + 1)
                if chain:
                    local_maxima(n, npar, half, between)
                sums(DV[2])
                if chain:
                    carries(n, npar, between)
                sums(DV[3])
                if chain:
                    maxima(n, npar, between)
                sums(DV[4])
                if chain:
                    weight(n, npar)
                for q in range(DG):
                    if chain:
                        weigh(npar, q)
                    between()
                sums(TB)

            v.memset(R[:, :, :], -BIG).then_inc(vec, 1)
            v.memset(arow[:, :, :], -BIG).then_inc(vec, 1)
            v.wait_ge(vec, 2)
            v.sem_inc(z_ready, 1)
            v.sem_inc(max_copied, 1)
            v.sem_inc(added, 4)
            onehots(0, first=True)
            over_batches(v, NB, step)
            v.wait_ge(added, NB * TB + 4)


class At:

    def __init__(self, turn, k):
        self.turn, self.k = turn, k
        self.n = turn * 2 + k
        self.par = k % 2
        self.half = turn + k // 2

    def plus(self, d):
        return At(self.turn, self.k + d)


def steps(eng, first, loop_first, loop_end, end, step):
    for n in range(first, loop_first):
        step(At(0, n), n)
    turns = max(0, (loop_end - loop_first) // 2)
    if turns:
        with eng.Fori(0, turns) as turn:
            for k in (0, 1):
                step(At(turn, loop_first + k), None)
    for n in range(loop_first + 2 * turns, end):
        step(At(0, n), n)


def edge_scan(nc, s, io, dr):
    GT = 32
    GE = GT * P
    CH = 512
    NC = GE // CH
    NG = s.ET // GT
    PT = 2
    with stage(nc, "edge_scan") as (c, sem):
        sb = lambda n, sh, dt=F32: c.enter_context(nc.sbuf_tensor(n, sh, dt))
        ea = sb("ea", [EF, 2, GE])
        run = sb("run", [EF, 2, 2, GE])
        out = sb("out_rows", [P, 2, GT, 2 * EF])
        keeps = sb("keeps", [1, 2, 2, GE], BF16)
        ones = sb("ones_ef", [1, EF], BF16)
        ident = c.enter_context(nc.sbuf_tensor("ident_ef", [P, P], F32))
        ident_i = c.enter_context(nc.sbuf_tensor("ident_efi", [P, P], I32))
        pK = [[c.enter_context(nc.psum_tensor(f"pK{m}{i}", [EF, CH], F32)) for i in range(2)] for m in range(2)]
        pR = [c.enter_context(nc.psum_tensor(f"pR{i}", [P, PT, 2 * EF], F32)) for i in range(4)]
        ea_in = [sem("ea_in0"), sem("ea_in1")]
        stored = [sem("rows_stored0"), sem("rows_stored1")]
        setup, masked, scanned, turned, copied, summed = (sem("setup"), sem("masked"), sem("scanned"), sem("turned"),
                                                          sem("copied"), sem("summed"))
        passed = sem("passed")
        block = c.enter_context(nc.Block())
        loop_end = 2 + max(0, (NG - 2 - 2) // 2) * 2
        RPC = CH // P // PT

        @block.sync
        def _(sp):
            def load(at):
                sp.dma_start(ea[:, at.par, :], io["ea_t"][:, bass.ds(at.n * GE, GE)]).then_inc(ea_in[at.par], 16)
                for m, name in enumerate(("keep_sum", "keep_max")):
                    sp.dma_start(keeps[:, at.par, m, :],
                                 dr[name].rearrange("(g e) -> g e", e=GE)[bass.ds(at.n, 1), :]).then_inc(ea_in[at.par], 16)

            def step(at, n):
                if n is None or n + 2 < NG:
                    sp.wait_ge(scanned, at.n * NC + (NC + 2))
                    load(at.plus(2))
                sp.wait_ge(copied, at.n * (NC * RPC) + (NC * RPC + 4))
                sp.dma_start(dr["rows"].rearrange("(g k p) f -> g p k f", p=P, k=GT)[bass.ds(at.n, 1), :, :, :]
                             .rearrange("o p k f -> (o p) k f"), out[:, at.par, :, :]).then_inc(stored[at.par], 16)

            load(At(0, 0))
            load(At(0, 1))
            steps(sp, 0, 2, loop_end, NG, step)
            sp.wait_ge(stored[0], 16 * ((NG + 1) // 2))
            sp.wait_ge(stored[1], 16 * (NG // 2))

        @block.gpsimd
        def _(g):
            g.memset(ones[:, :], 1.0).then_inc(setup, 1)
            g.iota(ident_i[:, :], pattern=[[1, P]], base=0, channel_multiplier=-1).then_inc(setup, 1)
            g.wait_ge(setup, 2)

        @block.tensor
        def _(pe):
            def turn_rows(at, i):
                pe.wait_ge(scanned, at.n * NC + (i + 3))
                pe.sem_inc(passed, 1)
                for r in range(RPC):
                    pe.wait_ge(copied, at.n * (NC * RPC) + (i * RPC + r + 1))
                    pe.sem_inc(passed, 1)
                    for k in range(PT):
                        e0 = i * CH + (r * PT + k) * P
                        for m in range(2):
                            mm = pe.transpose(pR[(i * RPC + r) % 4][:, k, m * EF:(m + 1) * EF],
                                              run[:, at.par, m, e0:e0 + P], ident[0:EF, 0:EF])
                    mm.then_inc(turned, 1)

            def step(at, n):
                pe.wait_ge(ea_in[at.par], at.half * 48 + 48)
                for i in range(NC):
                    pe.wait_ge(scanned, at.n * NC + (i + 1))
                    pe.sem_inc(passed, 1)
                    for m in range(2):
                        mm = pe.matmul(pK[m][i % 2][:, :], ones[:, :], keeps[:, at.par, m, i * CH:(i + 1) * CH],
                                       start=True, stop=True)
                    mm.then_inc(masked, 1)
                    if n != 0 or i:
                        turn_rows(at.plus(-1) if i == 0 else at, (i - 1) % NC)

            pe.wait_ge(setup, 3)
            pe.sem_inc(turned, 2 * NC * RPC)
            steps(pe, 0, 2, loop_end, NG, step)
            turn_rows(At(0, NG - 1), NC - 1)

        @block.scalar
        def _(a):
            def step(at, n):
                for q in range(NC * RPC):
                    a.wait_ge(turned, at.n * (NC * RPC) + (q + 1 + 2 * NC * RPC))
                    if q == 0 and (n is None or n >= 2):
                        a.wait_ge(stored[at.par], at.half * 16)
                    a.activation(out[:, at.par, q * PT:(q + 1) * PT, :], pR[q % 4][:, :, :], ACT.Copy).then_inc(copied, 1)

            a.sem_inc(copied, 4)
            steps(a, 0, 2, loop_end, NG, step)

        @block.vector
        def _(v):
            def step(at, n):
                for i in range(NC):
                    cols = slice(i * CH, (i + 1) * CH)
                    v.wait_ge(masked, at.n * NC + (i + 1))
                    if i == 0:
                        v.wait_ge(ea_in[at.par], at.half * 48 + 48)
                    v.wait_ge(turned, at.n * (NC * RPC) + ((i + 1) * RPC))
                    v.wait_ge(scanned, at.n * NC + (i + 2))
                    src, lastc = (at.par, i * CH - 1) if i else (1 - at.par, GE - 1)
                    v.tensor_tensor_scan(run[:, at.par, 0, cols], pK[0][i % 2][:, :], ea[:, at.par, cols],
                                         run[:, src, 0, lastc:lastc + 1], ALU.mult, ALU.add)
                    v.tensor_tensor_scan(run[:, at.par, 1, cols], pK[1][i % 2][:, :], ea[:, at.par, cols],
                                         run[:, src, 1, lastc:lastc + 1], ALU.add, ALU.max).then_inc(scanned, 1)

            v.memset(run[:, 1, :, GE - 1:GE], 0.0).then_inc(summed, 1)
            v.wait_ge(setup, 2)
            v.tensor_scalar(ident[:, :], ident_i[:, :], 0.0, None, ALU.is_equal).then_inc(setup, 1)
            v.wait_ge(summed, 1)
            v.sem_inc(scanned, 2)
            steps(v, 0, 2, loop_end, NG, step)
            v.wait_ge(scanned, NG * NC + 2)


LN_EPS = 1e-5


def project_attention(v, chain, weights, att, tmp, H):
    for k in range(2):
        for m in range(2):
            chain(v.tensor_tensor(tmp[:, :], weights[:, k, 0:XF], att[:, m, :], ALU.mult))
            chain(v.tensor_reduce(weights[:, k, XF + m * H:XF + (m + 1) * H],
                                  tmp[:, :].rearrange("p (h d) -> p h d", h=H), AX.X, ALU.add))


def node_mlp(nc, s, io, dr, keep):
    NT, NS = s.NT, s.NT // 2
    HID = io["w1"].shape[1]
    HC = HID // P
    GF = io["u"].shape[1]
    H = 4
    WG = XF + 2 * H
    N2 = 2 * P
    with stage(nc, "node_mlp") as (c, sem):
        sb = lambda n, sh, dt=F32: c.enter_context(nc.sbuf_tensor(n, sh, dt))
        pb = lambda n: c.enter_context(nc.psum_tensor(n, [P, 512], F32))
        w1h = sb("w1h", [P, 2, HID])
        w1e = sb("w1e", [EF, 3, HID])
        w1u = sb("w1u", [GF, HID])
        w2 = sb("w2", [P, HC, XF])
        b1 = sb("b1", [P, HC])
        b2 = sb("b2", [P, XF])
        u0 = sb("u0", [GF, 1])
        wg = sb("wg", [P, 2, WG])
        att = sb("att", [P, 2, XF])
        tmp = sb("tmp_att", [P, XF])
        has = sb("has", [P, NT])
        inv = sb("inv", [P, NT])
        x = sb("x_rows", [P, 2, 2, XF])
        agg = sb("agg_rows", [P, 2, 2, 2 * EF])
        idx = sb("idx_agg", [P, 2, 2], I32)
        hrow = sb("h_rows", [P, 2, 2, XF])
        feat = sb("feat", [P, 2, 2, 3 * EF])
        res = sb("res", [P, 2, 2, XF])
        hT = sb("hT", [P, 2, 2, N2])
        fT = sb("fT", [EF, 2, 3, N2])
        hid = sb("hid", [P, 2, HC, N2])
        x1 = sb("x1_rows", [P, 2, 2, XF])
        h1 = sb("h1_rows", [P, 2, XF])
        h1T = sb("h1T", [P, 2, 2, P])
        grow = sb("g_rows", [P, 2, 2, XF + H])
        st = sb("bn_st", [P, 2, 2, 6])
        mv = sb("bn_mv", [P, 2, 2, 2])
        var = sb("var", [P, 2, 2])
        root = sb("root", [P, 2, 2])
        rstd = sb("rstd", [P, 2, 2])
        nb = sb("nb", [P, 2, 2])
        pHT, pF0, pF1, pM2, pG, pGo = pb("pHT"), pb("pF0"), pb("pF1"), pb("pM2"), pb("pG_"), pb("pGo")
        pM1 = [pb("pM1a"), pb("pM1b")]
        x_in = [sem("x_in0"), sem("x_in1")]
        agg_in = [sem("agg_in0"), sem("agg_in1")]
        x1_out = [sem("x1_out0"), sem("x1_out1")]
        g_out = [sem("g_out0"), sem("g_out1")]
        w_in, ready, vec, bias_ready, idx_ready = sem("w_in"), sem("ready_c"), sem("vec_c"), sem("bias_ready"), sem("idx_ready")
        var_ready = [sem("var_ready0"), sem("var_ready1")]
        root_ready = [sem("root_ready0"), sem("root_ready1")]
        nb_ready = [sem("nb_ready0"), sem("nb_ready1")]
        stats = [sem("stats0"), sem("stats1")]
        summed = sem("summed_c")
        h_ready, h1_ready, feat_ready, res_ready = sem("h_ready"), sem("h1_ready"), sem("feat_ready"), sem("res_ready")
        t_ready, t_copied, m1_ready, m1_copied = sem("t_ready"), sem("t_copied"), sem("m1_ready"), sem("m1_copied")
        m2_ready, x1_ready, gt_ready, gt_copied = sem("m2_ready"), sem("x1_ready"), sem("gt_ready"), sem("gt_copied")
        go_ready, go_copied = sem("go_ready"), sem("go_copied")
        passed, passed_pe, passed_v = sem("passed_pool"), sem("passed_pe"), sem("passed_vector")
        block = c.enter_context(nc.Block())
        LOOP = 3
        LOOP_END = LOOP + max(0, (NS - 2 - LOOP) // 2) * 2
        xv = io["x"].rearrange("(s t p) f -> s p t f", p=P, t=2)
        x1v = dr["x1"].rearrange("(s t p) f -> s p t f", p=P, t=2)
        gv = dr["table1"].rearrange("(s t p) f -> s p t f", p=P, t=2)
        tile2 = lambda view, n: view[bass.ds(n, 1), :, :, :].rearrange("o p t f -> (o p) t f")

        def all_steps(eng, step, first=-1):
            steps(eng, first, LOOP, LOOP_END, NS + 1, step)

        @block.sync
        def _(sp):
            sp.dma_start(w1h[:, :, :], io["w1"][0:XF, :].rearrange("(k p) n -> p k n", p=P)).then_inc(w_in, 16)
            sp.dma_start(w1e[:, :, :], io["w1"][XF:XF + 3 * EF, :].rearrange("(k p) n -> p k n", p=EF)).then_inc(w_in, 16)
            sp.dma_start(w1u[:, :], io["w1"][XF + 3 * EF:XF + 3 * EF + GF, :]).then_inc(w_in, 16)
            sp.dma_start(w2[:, :, :], io["w2"].rearrange("(k p) n -> p k n", p=P)).then_inc(w_in, 16)
            sp.dma_start(b1[:, :], io["b1"].rearrange("(k p) -> p k", p=P), allow_slow_non_contiguous=True).then_inc(w_in, 16)
            sp.dma_start(b2[:, :], io["b2"].unsqueeze(0).to_broadcast([P, XF])).then_inc(w_in, 16)
            sp.dma_start(u0[:, :], io["u"][0:1, :].rearrange("o f -> f o"), allow_slow_non_contiguous=True).then_inc(w_in, 16)
            sp.dma_start(wg[:, :, 0:XF], io["g1_w"].rearrange("(k p) n -> p k n", p=P)).then_inc(w_in, 16)
            for m, name in enumerate(("g1_src", "g1_dst")):
                sp.dma_start(att[:, m, :], io[name].rearrange("h d -> (h d)").unsqueeze(0)
                             .to_broadcast([P, XF])).then_inc(w_in, 16)

            def step(at, n):
                if n is None or n + 2 < NS:
                    if n is None or n >= 0:
                        sp.wait_ge(res_ready, at.n + 1)
                    nxt = at.plus(2)
                    if n is None or n + 2 >= 1:
                        sp.dma_start(x[:, nxt.par, :, :], tile2(xv, nxt.n)).then_inc(x_in[nxt.par], 16)
                prev = at.plus(-1)
                if n is None or n >= 1:
                    sp.wait_ge(x1_ready, prev.n + 2)
                    sp.dma_start(tile2(x1v, prev.n), x1[:, prev.par, :, :]).then_inc(x1_out[prev.par], 16)
                    sp.wait_ge(go_copied, prev.n * 2 + 3)
                    sp.dma_start(tile2(gv, prev.n), grow[:, prev.par, :, :]).then_inc(g_out[prev.par], 16)

            sp.dma_start(x[:, 0, :, :], tile2(xv, 0)).then_inc(x_in[0], 16)
            all_steps(sp, step)
            for q in (x1_out, g_out):
                sp.wait_ge(q[0], 16 * ((NS + 1) // 2))
                sp.wait_ge(q[1], 16 * (NS // 2))

        @block.gpsimd
        def _(g):
            def step(at, n):
                if n is not None and n >= NS:
                    return
                if n is None or n >= 2:
                    g.wait_ge(feat_ready, at.n - 1)
                g.tensor_copy(idx[:, at.par, :], keep["end_i"][:, bass.ds(at.n * 2, 2)]).then_inc(idx_ready, 1)
                g.wait_ge(idx_ready, at.n + 1)
                g.sem_inc(passed, 1)
                for t in range(2):
                    g.indirect_dma_start(
                        out=agg[:, at.par, t, :], out_offset=None, in_=dr["rows"],
                        in_offset=bass.IndirectOffsetOnAxis(ap=idx[:, at.par, t:t + 1], axis=0),
                    ).then_inc(agg_in[at.par], 16)

            all_steps(g, step, first=0)

        @block.tensor
        def _(pe):
            pe.wait_ge(w_in, 16 * 10)
            for k in range(HC):
                mm = pe.matmul(pM1[0][:, k:k + 1], w1u[:, k * P:(k + 1) * P], u0[:, :], start=True, stop=True,
                               skip_group_check=True)
            mm.then_inc(bias_ready, 1)
            pe.wait_ge(ready, 1)

            def step(at, n):
                nxt, prev = at.plus(1), at.plus(-1)
                mlp = n is None or 0 <= n < NS
                if mlp:
                    pe.wait_ge(t_copied, at.n + 2)
                    for k in range(HC):
                        pe.wait_ge(m1_copied, at.n * HC + (k + 1))
                        cols = slice(k * P, (k + 1) * P)
                        out = pM1[k % 2][:, 0:N2]
                        for i in range(2):
                            pe.matmul(out, w1h[:, i, cols], hT[:, at.par, i, :], start=(i == 0), stop=False)
                        for i in range(3):
                            mm = pe.matmul(out, w1e[:, i, cols], fT[:, at.par, i, :], start=False, stop=(i == 2))
                        mm.then_inc(m1_ready, 1)
                if n is None or n >= 1:
                    for t in range(2):
                        pe.wait_ge(h1_ready, prev.n * 2 + (t + 1))
                        pe.wait_ge(gt_copied, prev.n * 2 + (t + 1))
                        for i in range(2):
                            mm = pe.transpose(pG[:, i * P:(i + 1) * P], h1[:, t, i * P:(i + 1) * P], keep["ident"][:, :])
                        mm.then_inc(gt_ready, 1)
                        pe.wait_ge(gt_copied, prev.n * 2 + (t + 2))
                        pe.wait_ge(go_copied, prev.n * 2 + (t + 1))
                        for i in range(2):
                            mm = pe.matmul(pGo[:, 0:WG], h1T[:, t, i, :], wg[:, i, :], start=(i == 0), stop=(i == 1))
                        mm.then_inc(go_ready, 1)
                if n is None or n + 1 < NS:
                    pe.wait_ge(h_ready, nxt.n * 2 + 2)
                    pe.wait_ge(feat_ready, nxt.n + 1)
                    pe.wait_ge(t_copied, nxt.n + 1)
                    pe.sem_inc(passed_pe, 1)
                    for t in range(2):
                        for i in range(2):
                            pe.transpose(pHT[:, i * N2 + t * P:i * N2 + (t + 1) * P],
                                         hrow[:, nxt.par, t, i * P:(i + 1) * P], keep["ident"][:, :])
                        for i in range(3):
                            out = (pF0, pF0, pF1)[i][0:EF, (i % 2) * N2 + t * P:(i % 2) * N2 + (t + 1) * P]
                            mm = pe.transpose(out, feat[:, nxt.par, t, i * EF:(i + 1) * EF], keep["ident"][:, :])
                    mm.then_inc(t_ready, 1)
                if mlp:
                    pe.wait_ge(m1_copied, at.n * HC + (HC + 2))
                    pe.wait_ge(x1_ready, at.n + 1)
                    for t in range(2):
                        for k in range(HC):
                            mm = pe.matmul(pM2[:, t * XF:(t + 1) * XF], hid[:, at.par, k, t * P:(t + 1) * P], w2[:, k, :],
                                           start=(k == 0), stop=(k == HC - 1), skip_group_check=True)
                    mm.then_inc(m2_ready, 1)

            all_steps(pe, step)

        @block.scalar
        def _(a):
            def hidden(at, ks):
                for k in ks:
                    a.wait_ge(m1_ready, at.n * HC + (k + 1))
                    a.activation(hid[:, at.par, k, :], pM1[k % 2][:, 0:N2], ACT.Relu,
                                 bias=b1[:, k:k + 1]).then_inc(m1_copied, 1)

            def roots(at, w):
                a.wait_ge(var_ready[w], at.n + 1)
                a.activation(root[:, w, :], var[:, w, :], ACT.Sqrt).then_inc(root_ready[w], 1)

            def normal(at, w, src, dst, done):
                a.wait_ge(nb_ready[w], at.n + 1)
                for t in range(2):
                    a.activation(dst[:, t, :], src[:, t, :], ACT.Relu, bias=nb[:, w, t:t + 1],
                                 scale=rstd[:, w, t:t + 1]).then_inc(done, 1)

            def step(at, n):
                nxt, prev = at.plus(1), at.plus(-1)
                mlp = n is None or 0 <= n < NS
                if mlp:
                    hidden(at, (0, 1))
                if n is None or n >= 1:
                    roots(prev, 1)
                if mlp:
                    hidden(at, (2,))
                if n is None or n >= 1:
                    normal(prev, 1, x1[:, prev.par, :, :], h1[:, :, :], h1_ready)
                if n is None or n + 1 < NS:
                    roots(nxt, 0)
                if mlp:
                    hidden(at, (3, 4))
                if n is None or n + 1 < NS:
                    normal(nxt, 0, x[:, nxt.par, :, :], hrow[:, nxt.par, :, :], h_ready)
                if mlp:
                    hidden(at, range(5, HC))

            a.wait_ge(ready, 1)
            a.sem_inc(m1_copied, 2)
            all_steps(a, step)

        @block.vector
        def _(v):
            chain = Chain(v, vec)
            v.wait_ge(w_in, 16 * 10)
            project_attention(v, chain, wg, att, tmp, H)
            chain(v.tensor_scalar(has[:, :], keep["cnt"][:, :], 1.0, None, ALU.min))
            chain(v.tensor_scalar(inv[:, :], keep["cnt"][:, :], 1.0, None, ALU.max))
            chain(v.reciprocal(inv[:, :], inv[:, :]))
            chain(v.tensor_tensor(inv[:, :], inv[:, :], has[:, :], ALU.mult))
            v.wait_ge(bias_ready, 1)
            chain(v.tensor_tensor(b1[:, :], b1[:, :], pM1[0][:, 0:HC], ALU.add))
            v.sem_inc(ready, 1)

            def statistics(at, w, src):
                base = at.n * 5
                for t in range(2):
                    v.bn_stats(st[:, w, t, :], src[:, t, :]).then_inc(stats[w], 1)
                v.wait_ge(stats[w], base + 2)
                v.sem_inc(passed_v, 1)
                for t in range(2):
                    v.bn_aggr(mv[:, w, t, :], st[:, w, t, :]).then_inc(stats[w], 1)
                v.wait_ge(stats[w], base + 4)
                v.tensor_scalar(var[:, w, :].unsqueeze(2), mv[:, w, :, 1:2], LN_EPS, None, ALU.add).then_inc(var_ready[w], 1)

            def inverse(at, w):
                v.wait_ge(root_ready[w], at.n + 1)
                v.reciprocal(rstd[:, w, :], root[:, w, :]).then_inc(stats[w], 1)
                v.wait_ge(stats[w], at.n * 5 + 5)
                v.scalar_tensor_tensor(out=nb[:, w, :].unsqueeze(2), in0=mv[:, w, :, 0:1], scalar=-1.0,
                                       in1=rstd[:, w, :].unsqueeze(2), op0=ALU.mult, op1=ALU.mult).then_inc(nb_ready[w], 1)

            def result(at, n):
                if n is None or n >= 2:
                    v.wait_ge(x1_out[at.par], at.half * 16)
                v.wait_ge(m2_ready, at.n + 1)
                v.tensor_tensor(x1[:, at.par, :, :], res[:, at.par, :, :],
                                pM2[:, :].rearrange("p (t f) -> p t f", t=2), ALU.add).then_inc(x1_ready, 1)
                v.wait_ge(x1_ready, at.n + 2)
                statistics(at, 1, x1[:, at.par, :, :])

            def features(at):
                v.wait_ge(agg_in[at.par], at.half * 32 + 32)
                for t in range(2):
                    j = at.n * 2 + t
                    v.tensor_scalar(feat[:, at.par, t, 0:2 * EF], agg[:, at.par, t, :],
                                    has[:, bass.ds(j, 1)], None, ALU.mult)
                    ins = v.tensor_scalar(feat[:, at.par, t, 2 * EF:3 * EF], agg[:, at.par, t, 0:EF],
                                          inv[:, bass.ds(j, 1)], None, ALU.mult)
                ins.then_inc(feat_ready, 1)

            def residual(at):
                v.wait_ge(h_ready, at.n * 2 + 2)
                v.tensor_tensor(res[:, at.par, :, :], x[:, at.par, :, :], hrow[:, at.par, :, :], ALU.add).then_inc(summed, 1)
                v.wait_ge(summed, at.n + 1)
                v.tensor_tensor(res[:, at.par, :, :], res[:, at.par, :, :],
                                b2[:, :].unsqueeze(1).to_broadcast([P, 2, XF]), ALU.add).then_inc(res_ready, 1)

            def step(at, n):
                nxt, prev = at.plus(1), at.plus(-1)
                back = n is None or n >= 1
                front = n is None or n + 1 < NS
                if back:
                    result(prev, None if n is None else n - 1)
                if front:
                    v.wait_ge(x_in[nxt.par], nxt.half * 16 + 16)
                    statistics(nxt, 0, x[:, nxt.par, :, :])
                if back:
                    inverse(prev, 1)
                if front:
                    inverse(nxt, 0)
                    features(nxt)
                    residual(nxt)
                if back:
                    for t in range(2):
                        v.wait_ge(gt_ready, prev.n * 2 + (t + 1))
                        v.tensor_copy(h1T[:, t, :, :].rearrange("p i n -> p (i n)"), pG[:, 0:N2]).then_inc(gt_copied, 1)
                        v.wait_ge(go_ready, prev.n * 2 + (t + 1))
                        if t == 0 and (n is None or n >= 3):
                            v.wait_ge(g_out[prev.par], prev.half * 16)
                        v.tensor_copy(keep["ald"][:, bass.ds(prev.n * 2 + t, 1), :].rearrange("p o h -> p (o h)"),
                                      pGo[:, XF + H:WG])
                        v.tensor_copy(keep["als"][:, bass.ds(prev.n * 2 + t, 1), :].rearrange("p o h -> p (o h)"),
                                      pGo[:, XF:XF + H])
                        v.tensor_copy(grow[:, prev.par, t, :], pGo[:, 0:XF + H]).then_inc(go_copied, 1)
                if front:
                    v.wait_ge(t_ready, nxt.n + 1)
                    v.tensor_copy(hT[:, nxt.par, :, :].rearrange("p i n -> p (i n)"), pHT[:, :])
                    v.tensor_copy(fT[:, nxt.par, 0:2, :].rearrange("p i n -> p (i n)"), pF0[0:EF, :])
                    v.tensor_copy(fT[:, nxt.par, 2, :], pF1[0:EF, 0:N2]).then_inc(t_copied, 1)

            v.sem_inc(t_copied, 1)
            v.sem_inc(x1_ready, 1)
            v.sem_inc(gt_copied, 1)
            v.sem_inc(go_copied, 1)
            all_steps(v, step)


def open_layer(nc, s, H, keep, adt):
    NT = s.NT
    with stage(nc, f"open_layer{H}") as (c, sem):
        rest = c.enter_context(nc.sbuf_tensor(f"rest{H}", [P, NT, H], F32))
        vec = sem("vec_o")
        block = c.enter_context(nc.Block())

        @block.vector
        def _(v):
            chain = Chain(v, vec)
            ald = keep["ald"][:, :, 0:H]
            chain(v.tensor_copy(adt[:, :, 0, :], ald))
            chain(v.tensor_tensor(rest[:, :, :], ald, adt[:, :, 0, :], ALU.subtract))
            chain(v.tensor_copy(adt[:, :, 1, :], rest[:, :, :]))
            chain(v.tensor_tensor(rest[:, :, :], rest[:, :, :], adt[:, :, 1, :], ALU.subtract))
            chain(v.tensor_copy(adt[:, :, 2, :], rest[:, :, :]))


def close_layer(nc, s, H, io, dr, keep, acc, last):
    NT = s.NT
    D = XF // H
    WG = XF + 2
    table = dr["table2"] if last else dr["table1"]
    bias_in = io["g2_b"] if last else io["g1_b"]
    with stage(nc, f"close_layer{H}") as (c, sem):
        sb = lambda n, sh, dt=F32: c.enter_context(nc.sbuf_tensor(f"{n}_cl{H}", sh, dt))
        pb = lambda n: c.enter_context(nc.psum_tensor(f"{n}_cl{H}", [P, 512], F32))
        es = sb("es", [P, NT, H])
        m = sb("m", [P, NT, H])
        top = sb("top", [P, NT, H])
        ga = sb("ga", [P, NT, H])
        gb = sb("gb", [P, NT, H])
        den = sb("den", [P, NT, H])
        none = sb("none", [P, NT])
        bias = sb("bias", [P, XF])
        hrow = sb("hrow", [P, 2, XF])
        xrow = sb("xrow", [P, 2, XF])
        own = sb("own", [P, 2, XF])
        t1 = sb("t1", [P, XF])
        y = sb("y", [P, 2, XF])
        mn = sb("mn", [P, 2, XF])
        ex = sb("ex", [P, 2, XF])
        rl = sb("rl", [P, 2, XF])
        h2 = sb("h2", [P, 2, XF])
        h2T = sb("h2T", [P, 2, 2, P])
        grow = sb("grow", [P, 2, XF + 1])
        zero = sb("zero", [P, XF + 8])
        wg = sb("wg", [P, 2, WG])
        att = sb("att", [P, 2, XF])
        pT = [pb("pT0"), pb("pT1")]
        pO = [pb("pO0"), pb("pO1")]
        own_in = [sem("own_in0"), sem("own_in1")]
        out_done = [sem("out_done0"), sem("out_done1")]
        w_in, vec, e_ready, e_done, own_ready = sem("w_in_l"), sem("vec_l"), sem("e_ready"), sem("e_done"), sem("own_ready")
        y_steps, y_ready, elu_ready, cleared, h2_ready = sem("y_steps"), sem("y_ready"), sem("elu_ready"), sem("cleared"), sem("h2_ready")
        t_ready, t_copied, o_ready, o_copied = sem("t_ready_l"), sem("t_copied_l"), sem("o_ready"), sem("o_copied")
        block = c.enter_context(nc.Block())
        LOOP = 4
        LOOP_END = LOOP + max(0, (NT - 2 - LOOP) // 2) * 2
        tv = table.rearrange("(j p) f -> j p f", p=P)
        xv = dr["x1"].rearrange("(j p) f -> j p f", p=P)
        ov = (io["out"] if last else dr["table2"]).rearrange("(j p) f -> j p f", p=P)
        END = NT if last else NT + 2
        at_tile = lambda view, n: view[bass.ds(n, 1), :, :].rearrange("o p f -> (o p) f")

        @block.sync
        def _(sp):
            sp.dma_start(bias[:, :], bias_in.unsqueeze(0).to_broadcast([P, XF])).then_inc(w_in, 16)
            if not last:
                sp.dma_start(wg[:, :, 0:XF], io["g2_w"].rearrange("(k p) n -> p k n", p=P)).then_inc(w_in, 16)
                for q, name in enumerate(("g2_src", "g2_dst")):
                    sp.dma_start(att[:, q, :], io[name].rearrange("h d -> (h d)").unsqueeze(0)
                                 .to_broadcast([P, XF])).then_inc(w_in, 16)

            def load(at):
                sp.dma_start(hrow[:, at.par, :], at_tile(tv, at.n)[:, 0:XF]).then_inc(own_in[at.par], 16)
                if last:
                    sp.dma_start(xrow[:, at.par, :], at_tile(xv, at.n)).then_inc(own_in[at.par], 16)

            def step(at, n):
                if last or n is None or n < NT:
                    sp.wait_ge(y_ready, at.n + 1)
                if n is None or n + 2 < NT:
                    load(at.plus(2))
                if last:
                    sp.dma_start(at_tile(ov, at.n), y[:, at.par, :]).then_inc(out_done[at.par], 16)
                elif n is None or n >= 2:
                    prev = at.plus(-2)
                    sp.wait_ge(o_copied, prev.n + 1)
                    sp.dma_start(at_tile(ov, prev.n), grow[:, prev.par, :]).then_inc(out_done[prev.par], 16)

            load(At(0, 0))
            load(At(0, 1))
            steps(sp, 0, LOOP, LOOP_END, END, step)
            sp.wait_ge(out_done[0], 16 * ((NT + 1) // 2))
            sp.wait_ge(out_done[1], 16 * (NT // 2))

        @block.gpsimd
        def _(g):
            def step(at, n):
                if n is not None and n >= NT:
                    return
                loads = 32 if last else 16
                g.wait_ge(own_in[at.par], at.half * loads + loads)
                if n is None or n >= 2:
                    g.wait_ge(y_ready, at.n - 1)
                g.tensor_tensor(own[:, at.par, :].rearrange("p (h d) -> p h d", h=H),
                                hrow[:, at.par, :].rearrange("p (h d) -> p h d", h=H),
                                gb[:, bass.ds(at.n, 1), :].rearrange("p o h -> p (o h)").unsqueeze(2)
                                .to_broadcast([P, H, D]), ALU.mult).then_inc(own_ready, 1)

            g.memset(zero[:, :], 0.0).then_inc(cleared, 1)
            g.wait_ge(e_ready, 2)
            steps(g, 0, LOOP, LOOP_END, END, step)

        @block.tensor
        def _(pe):
            def step(at, n):
                if n is not None and not 1 <= n <= NT:
                    return
                prev = at.plus(-1)
                pe.wait_ge(h2_ready, prev.n + 1)
                for i in range(2):
                    mm = pe.transpose(pT[prev.par][:, i * P:(i + 1) * P], h2[:, prev.par, i * P:(i + 1) * P],
                                      keep["ident"][:, :])
                mm.then_inc(t_ready, 1)
                pe.wait_ge(t_copied, prev.n + 1)
                if n is None or n >= 3:
                    pe.wait_ge(o_copied, prev.n - 1)
                for i in range(2):
                    mm = pe.matmul(pO[prev.par][:, 0:WG], h2T[:, prev.par, i, :], wg[:, i, :], start=(i == 0), stop=(i == 1))
                mm.then_inc(o_ready, 1)

            if not last:
                pe.wait_ge(e_ready, 2)
                steps(pe, 0, LOOP, LOOP_END, END, step)

        @block.scalar
        def _(a):
            a.wait_ge(e_ready, 1)
            a.activation(ga[:, :, :], m[:, :, :], ACT.Exp).then_inc(e_done, 1)
            a.activation(gb[:, :, :], es[:, :, :], ACT.Exp).then_inc(e_done, 1)

            def step(at, n):
                if n is None or n < NT:
                    a.wait_ge(y_ready, at.n + 1)
                    a.activation(rl[:, at.par, :], y[:, at.par, :], ACT.Relu)
                    a.activation(ex[:, at.par, :], mn[:, at.par, :], ACT.Exp).then_inc(elu_ready, 1)
                    a.activation(acc[:, bass.ds(at.n, 1), :].rearrange("p o w -> p (o w)"), zero[:, :],
                                 ACT.Copy).then_inc(cleared, 1)
                if n is None or 1 <= n <= NT:
                    prev = at.plus(-1)
                    a.wait_ge(t_ready, prev.n + 1)
                    a.activation(h2T[:, prev.par, :, :].rearrange("p i n -> p (i n)"), pT[prev.par][:, 0:2 * P],
                                 ACT.Copy).then_inc(t_copied, 1)

            if not last:
                a.wait_ge(cleared, 1)
                steps(a, 0, LOOP, LOOP_END, END, step)
                a.wait_ge(cleared, NT + 1)

        @block.vector
        def _(v):
            chain = Chain(v, vec)
            cnt = keep["cnt"]
            als, ald = keep["als"][:, :, 0:H], keep["ald"][:, :, 0:H]
            v.wait_ge(w_in, 16 if last else 64)
            if not last:
                project_attention(v, chain, wg, att, t1, 1)
            chain(v.tensor_tensor(es[:, :, :], als, ald, ALU.add))
            chain(v.scalar_tensor_tensor(out=es[:, :, :], in0=es[:, :, :], scalar=0.2, in1=es[:, :, :],
                                         op0=ALU.mult, op1=ALU.max))
            chain(v.tensor_scalar(none[:, :], cnt[:, :], 0.0, -BIG, ALU.is_equal, ALU.mult))
            chain(v.tensor_tensor(m[:, :, :], acc[:, :, XF + H:XF + 2 * H],
                                  none[:, :].unsqueeze(2).to_broadcast([P, NT, H]), ALU.add))
            chain(v.tensor_tensor(top[:, :, :], m[:, :, :], es[:, :, :], ALU.max))
            chain(v.tensor_tensor(m[:, :, :], m[:, :, :], top[:, :, :], ALU.subtract))
            chain(v.tensor_tensor(es[:, :, :], es[:, :, :], top[:, :, :], ALU.subtract))
            v.sem_inc(e_ready, 1)
            v.wait_ge(e_done, 2)
            chain(v.tensor_tensor(den[:, :, :], acc[:, :, XF:XF + H], ga[:, :, :], ALU.mult))
            chain(v.tensor_tensor(den[:, :, :], den[:, :, :], gb[:, :, :], ALU.add))
            chain(v.tensor_scalar(den[:, :, :], den[:, :, :], 1e-16, None, ALU.add))
            chain(v.reciprocal(den[:, :, :], den[:, :, :]))
            chain(v.tensor_tensor(ga[:, :, :], ga[:, :, :], den[:, :, :], ALU.mult))
            chain(v.tensor_tensor(gb[:, :, :], gb[:, :, :], den[:, :, :], ALU.mult))
            v.sem_inc(e_ready, 1)

            def output(at, n):
                K = 3
                def done(ins, k):
                    ins.then_inc(y_steps, 1)
                    v.wait_ge(y_steps, at.n * K + k)
                heads = lambda ap: ap.rearrange("p (h d) -> p h d", h=H)
                if last and (n is None or n >= 2):
                    v.wait_ge(out_done[at.par], at.half * 16)
                done(v.tensor_tensor(heads(t1[:, :]), heads(acc[:, bass.ds(at.n, 1), 0:XF].rearrange("p o f -> p (o f)")),
                                     ga[:, bass.ds(at.n, 1), :].rearrange("p o h -> p (o h)").unsqueeze(2)
                                     .to_broadcast([P, H, D]), ALU.mult), 1)
                v.wait_ge(own_ready, at.n + 1)
                done(v.tensor_tensor(y[:, at.par, :], t1[:, :], own[:, at.par, :], ALU.add), 2)
                done(v.tensor_tensor(y[:, at.par, :], y[:, at.par, :], bias[:, :], ALU.add), 3)
                if last:
                    v.tensor_tensor(y[:, at.par, :], y[:, at.par, :], xrow[:, at.par, :], ALU.add).then_inc(y_ready, 1)
                else:
                    v.tensor_scalar(mn[:, at.par, :], y[:, at.par, :], 0.0, None, ALU.min).then_inc(y_ready, 1)

            def step(at, n):
                if n is None or n < NT:
                    output(at, n)
                if last:
                    return
                if n is None or 1 <= n <= NT:
                    prev = at.plus(-1)
                    v.wait_ge(elu_ready, prev.n + 1)
                    v.scalar_tensor_tensor(out=h2[:, prev.par, :], in0=ex[:, prev.par, :], scalar=-1.0,
                                           in1=rl[:, prev.par, :], op0=ALU.add, op1=ALU.add).then_inc(h2_ready, 1)
                if n is None or n >= 2:
                    prev = at.plus(-2)
                    v.wait_ge(o_ready, prev.n + 1)
                    if n is None or n >= 4:
                        v.wait_ge(out_done[prev.par], prev.half * 16)
                    j = bass.ds(prev.n, 1)
                    v.tensor_copy(keep["als"][:, j, 0:1].rearrange("p o h -> p (o h)"), pO[prev.par][:, XF:XF + 1])
                    v.tensor_copy(keep["ald"][:, j, 0:1].rearrange("p o h -> p (o h)"), pO[prev.par][:, XF + 1:WG])
                    v.tensor_copy(grow[:, prev.par, :], pO[prev.par][:, 0:XF + 1]).then_inc(o_copied, 1)

            steps(v, 0, LOOP, LOOP_END, END, step)


def setup(nc, s, keep):
    with stage(nc, "setup") as (c, sem):
        diag = c.enter_context(nc.sbuf_tensor("diag", [P, P], I32))
        cols = c.enter_context(nc.sbuf_tensor("cols", [P, P], I32))
        filled = sem("filled")
        block = c.enter_context(nc.Block())

        @block.gpsimd
        def _(g):
            g.iota(diag[:, :], pattern=[[1, P]], base=0, channel_multiplier=-1).then_inc(filled, 1)
            g.iota(cols[:, :], pattern=[[1, P]], base=0, channel_multiplier=0).then_inc(filled, 1)
            g.memset(keep["ones"][:, :], 1.0).then_inc(filled, 1)
            g.wait_ge(filled, 3)

        @block.vector
        def _(v):
            v.wait_ge(filled, 3)
            v.tensor_scalar(keep["ident"][:, :], diag[:, :], 0.0, None, ALU.is_equal).then_inc(filled, 1)
            v.tensor_copy(keep["iota"][:, :], cols[:, :]).then_inc(filled, 1)
            v.tensor_scalar(keep["ident_b"][:, :], diag[:, :], 0.0, None, ALU.is_equal).then_inc(filled, 1)
            v.wait_ge(filled, 6)


def clear(nc, acc, NT):
    with stage(nc, "clear") as (c, sem):
        low, high = sem("cleared_low"), sem("cleared_high")
        block = c.enter_context(nc.Block())

        @block.gpsimd
        def _(g):
            g.memset(acc[:, 0:NT // 2, :], 0.0).then_inc(low, 1)
            g.wait_ge(low, 1)

        @block.vector
        def _(v):
            v.memset(acc[:, NT // 2:NT, :], 0.0).then_inc(high, 1)
            v.wait_ge(high, 1)


def gnn_layer_then_gat(nc, s, io):
    H1, H2 = io["g1_src"].shape[0], io["g2_src"].shape[0]
    dram = lambda n, sh, dt=F32: nc.dram_tensor(n, sh, dt).ap()
    dr = dict(keep_sum=dram("keep_sum_d", [s.EP], BF16), keep_max=dram("keep_max_d", [s.EP], BF16),
              tab=dram("tab_d", [s.NI, 5 * P]), rec=dram("rec_d", [s.NB, REC]), ends=dram("ends_d", [3, s.NI]),
              rows=dram("rows_d", [s.EP, 2 * EF]), x1=dram("x1_d", [s.NP, XF]),
              table1=dram("table1_d", [s.NP, XF + H1]), table2=dram("table2_d", [s.NP, XF + H2]))
    with ExitStack() as c:
        sb = lambda n, sh, dt=F32: c.enter_context(nc.sbuf_tensor(n, sh, dt))
        keep = dict(ident=sb("k_ident", [P, P]), ident_b=sb("k_ident_b", [P, P], BF16), iota=sb("k_iota", [P, P], BF16), ones=sb("k_ones", [P, 16]),
                    jrow=sb("k_jrow", [1, s.NI], I32), cnt=sb("k_cnt", [P, s.NT]), base=sb("k_base", [P, s.KT]),
                    end_i=sb("k_end", [P, s.NT], I32), rel=sb("k_rel", [P, s.NI], BF16),
                    last=sb("k_last", [P, s.NI], BF16), src=sb("k_src", [P, s.NI], I32),
                    als=sb("k_als", [P, s.NT, H1]), ald=sb("k_ald", [P, s.NT, H1]),
                    items_in=c.enter_context(nc.semaphore("items_in")))
        setup(nc, s, keep)
        with ExitStack() as c2:
            for name in ("D", "Nx", "S"):
                keep[name] = c2.enter_context(nc.sbuf_tensor(f"k_{name}", [P, s.KT, P], I32))
            structure(nc, s, io, dr, keep)
            masks(nc, s, dr, keep)
        edge_scan(nc, s, io, dr)
        node_mlp(nc, s, io, dr, keep)
        acc = sb("acc", [P, s.NT, XF + 2 * H1])
        clear(nc, acc, s.NT)
        for layer, H in ((1, H1), (2, H2)):
            with ExitStack() as c3:
                adt = c3.enter_context(nc.sbuf_tensor(f"adt{layer}", [P, s.NT, 3, H], BF16))
                open_layer(nc, s, H, keep, adt)
                attention(nc, s, H, keep, dr, dr[f"table{layer}"], acc, adt)
            close_layer(nc, s, H, io, dr, keep, acc, last=(layer == 2))


_NAMES = dict(L0_gnn_u="u", L0_gnn_W1="w1", L0_gnn_b1="b1", L0_gnn_W2="w2", L0_gnn_b2="b2",
              L1_gnn_W1="g1_w", L1_gnn_att_src1="g1_src", L1_gnn_att_dst1="g1_dst", L1_gnn_b1="g1_b",
              L1_gnn_W2="g2_w", L1_gnn_att_src2="g2_src", L1_gnn_att_dst2="g2_dst", L1_gnn_b2="g2_b")


def kernel(**inputs):
    import concourse.bacc as bacc
    from concourse.bass_utils import run_bass_kernel_spmd as run

    x, src, dst, ea = (np.asarray(inputs[k]) for k in ("x", "src", "dst", "edge_attr_96"))
    s = Shapes(x.shape[0], src.shape[0])
    around = np.full(s.EP + 2, PAD_NODE, np.int32)
    around[0] = -1
    around[1:s.E + 1] = dst
    arrays = dict(x=np.zeros((s.NP, XF), x.dtype), src=np.zeros(s.EP, src.dtype),
                  dst=around[1:-1].copy(), dst_prev=around[:-2].copy(), dst_next=around[2:].copy(),
                  ea_t=np.zeros((EF, s.EP), ea.dtype))
    arrays["x"][:s.N] = x
    arrays["src"][:s.E] = src
    arrays["ea_t"][:, :s.E] = ea.T
    for name, short in _NAMES.items():
        arrays[short] = np.ascontiguousarray(inputs[name])
    nc = bacc.Bacc("TRN2", target_bir_lowering=False, num_devices=1)
    io = {n: nc.dram_tensor(f"in_{n}", a.shape, mybir.dt.from_np(a.dtype), kind="ExternalInput").ap()
          for n, a in arrays.items()}
    io["out"] = nc.dram_tensor("out_x", (s.NP, XF), F32, kind="ExternalOutput").ap()
    gnn_layer_then_gat(nc, s, io)
    r = run(nc, [{f"in_{n}": a for n, a in arrays.items()}], core_ids=[0])
    return r.results[0]["out_x"][:s.N]
```
